# Optimizing a Trainium2 kernel written in Bass

```python
import numpy as np
import jax
import jax.numpy as jnp

def _softmax(x, axis=-1):
    return jax.nn.softmax(x, axis=axis)

def _gelu(x):
    return jax.nn.gelu(x, approximate=True)

def _silu(x):
    return jax.nn.silu(x)

def _sigmoid(x):
    return jax.nn.sigmoid(x)

def _layernorm(x, axis=-1, eps=1e-05):
    m = jnp.mean(x, axis=axis, keepdims=True)
    v = jnp.var(x, axis=axis, keepdims=True)
    return (x - m) / jnp.sqrt(v + eps)

def _scatter_add(tgt, idx, src, axis=0):
    return tgt.at[idx].add(src)

def _segment_sum(src, seg, n):
    return jax.ops.segment_sum(src, seg, n)
kernel_name = 'mk_gnn_resnorm_d4_gnn_r32_1a2684'

def setup_inputs(seed: int=0):
    np.random.seed(seed)
    _w = jnp.asarray

    def _rec_inputs():
        import jax
        import jax.numpy as jnp
        _gk = jax.random.key(seed)
        x = -0.0002117 + 1 * jax.random.normal(jax.random.fold_in(_gk, 1), (3125, 256), jnp.float32)
        src = jax.random.randint(jax.random.fold_in(_gk, 2), (50000,), 0, 3125, jnp.int32)
        dst = jax.random.randint(jax.random.fold_in(_gk, 3), (50000,), 0, 3125, jnp.int32)
        _o = jnp.argsort(dst, stable=True)
        src = src[_o]
        dst = dst[_o]
        edge_weight = jax.random.uniform(jax.random.fold_in(_gk, 13), (50000,), jnp.float32, 0.0, 1)
        node_vec = jax.random.uniform(jax.random.fold_in(_gk, 14), (3125,), jnp.float32, 0.0, 0.999884)
        return (x, src, dst, edge_weight, node_vec)
    x, src, dst, edge_weight, node_vec = _rec_inputs()

    def _L0_gnn_setup():
        import jax, jax.numpy as jnp
        import numpy as np
        N = 3125
        E = 100000
        F = 256
        C = 256
        key = jax.random.key(seed)
        k1, k2, k3, k4, k5 = jax.random.split(key, 5)
        x = jax.random.normal(k1, (N, F), dtype=jnp.float32)
        edge_row = jax.random.randint(k2, (E,), 0, N, dtype=jnp.int32)
        edge_col = jax.random.randint(k3, (E,), 0, N, dtype=jnp.int32)
        edge_vals = jax.random.uniform(k4, (E,), dtype=jnp.float32)
        kernel = jax.random.normal(k5, (F, C), dtype=jnp.float32) * (1.0 / np.sqrt(F))
        bias = jnp.zeros((C,), dtype=jnp.float32)
        return {'x': x, 'edge_row': edge_row, 'edge_col': edge_col, 'edge_vals': edge_vals, 'kernel': kernel, 'bias': bias}
    _L0_gnn_all = _L0_gnn_setup()
    _L0_gnn_in = {k: v for k, v in _L0_gnn_all.items() if k in ('kernel', 'bias')}
    del _L0_gnn_all

    def _L1_gnn_setup():
        import jax, jax.numpy as jnp
        import numpy as np
        N = 50000
        E = 25000
        IN_F = 256
        OUT_F = 64
        NHEAD = 4
        ALPHA = 0.2

        def _gat_forward(x, W, a_l, a_r, edge):
            n = x.shape[0]
            row, col = (edge[0], edge[1])
            h = (x @ W).reshape(n, NHEAD, OUT_F)
            hl = jnp.sum(a_l * h, axis=-1)
            hr = jnp.sum(a_r * h, axis=-1)
            e = jax.nn.leaky_relu(hl[row] + hr[col], negative_slope=ALPHA)
            e_max = jax.ops.segment_max(e, row, num_segments=n)
            e_max = jnp.where(jnp.isfinite(e_max), e_max, 0.0)
            ee = jnp.exp(e - e_max[row])
            denom = jax.ops.segment_sum(ee, row, num_segments=n)
            att = ee / denom[row]
            msg = att[:, :, None] * h[col]
            out_h = jax.ops.segment_sum(msg, row, num_segments=n)
            return out_h.reshape(n, NHEAD * OUT_F)
        key = jax.random.key(seed)
        k1, k2, k3, k4, k5 = jax.random.split(key, 5)
        x = jax.random.normal(k1, (N, IN_F), dtype=jnp.float32)
        edge = jax.random.randint(k2, (2, E), 0, N, dtype=jnp.int32)
        stdv_W = float(np.sqrt(6.0 / (IN_F + OUT_F * NHEAD)))
        W = jax.random.uniform(k3, (IN_F, OUT_F * NHEAD), jnp.float32, -stdv_W, stdv_W)
        stdv_a = float(np.sqrt(6.0 / (NHEAD + OUT_F)))
        a_l = jax.random.uniform(k4, (1, NHEAD, OUT_F), jnp.float32, -stdv_a, stdv_a)
        a_r = jax.random.uniform(k5, (1, NHEAD, OUT_F), jnp.float32, -stdv_a, stdv_a)
        return {'x': x, 'edge': edge, 'W': W, 'a_l': a_l, 'a_r': a_r}
    _L1_gnn_all = _L1_gnn_setup()
    _L1_gnn_in = {k: v for k, v in _L1_gnn_all.items() if k in ('W', 'a_l', 'a_r')}
    del _L1_gnn_all

    def _L2_gnn_setup():
        import jax, jax.numpy as jnp
        import numpy as np
        NUM_NODES = 50000
        NUM_EDGES = 50000
        NNZ = 15625
        D_IN = 256
        D_OUT = 256
        key = jax.random.key(seed)
        k1, k2, k3, k4, k5, k6 = jax.random.split(key, 6)
        x = jax.random.normal(k1, (NUM_NODES, D_IN), dtype=jnp.float32)
        node_idx = jax.random.randint(k2, (NNZ,), 0, NUM_NODES, dtype=jnp.int64)
        edge_idx = jax.random.randint(k3, (NNZ,), 0, NUM_EDGES, dtype=jnp.int64)
        hyperedge_index = jnp.stack([node_idx, edge_idx], axis=0)
        hyperedge_weight = jax.random.uniform(k4, (NUM_EDGES,), dtype=jnp.float32)
        W = jax.random.normal(k5, (D_IN, D_OUT), dtype=jnp.float32) / np.sqrt(D_IN)
        b = jax.random.normal(k6, (D_OUT,), dtype=jnp.float32) * 0.01
        return {'x': x, 'hyperedge_index': hyperedge_index, 'hyperedge_weight': hyperedge_weight, 'W': W, 'b': b}
    _L2_gnn_all = _L2_gnn_setup()
    _L2_gnn_in = {k: v for k, v in _L2_gnn_all.items() if k in ('W', 'b')}
    del _L2_gnn_all

    def _L3_gnn_setup():
        import jax, jax.numpy as jnp
        import numpy as np
        N, IN_CH, HEADS, OUT_CH, E = (50000, 256, 4, 64, 25000)
        key = jax.random.key(seed)
        k1, k2, k3, k4, k5 = jax.random.split(key, 5)
        x = jax.random.normal(k1, (N, IN_CH), dtype=jnp.float32)
        edge_index = jax.random.randint(k2, (2, E), 0, N, dtype=jnp.int64)
        bw = float(np.sqrt(6.0 / (IN_CH + HEADS * OUT_CH)))
        ba = float(np.sqrt(6.0 / (HEADS + OUT_CH)))
        weight = jax.random.uniform(k3, (IN_CH, HEADS * OUT_CH), jnp.float32, -bw, bw)
        attn_l = jax.random.uniform(k4, (HEADS, OUT_CH), jnp.float32, -ba, ba)
        attn_r = jax.random.uniform(k5, (HEADS, OUT_CH), jnp.float32, -ba, ba)
        return {'x': x, 'edge_index': edge_index, 'weight': weight, 'attn_l': attn_l, 'attn_r': attn_r}
    _L3_gnn_all = _L3_gnn_setup()
    _L3_gnn_in = {k: v for k, v in _L3_gnn_all.items() if k in ('weight', 'attn_l', 'attn_r')}
    del _L3_gnn_all
    return {'x': x, 'src': src, 'dst': dst, 'edge_weight': edge_weight, 'node_vec': node_vec, 'L0_gnn_kernel': _L0_gnn_in['kernel'], 'L0_gnn_bias': _L0_gnn_in['bias'], 'L1_gnn_W': _L1_gnn_in['W'], 'L1_gnn_a_l': _L1_gnn_in['a_l'], 'L1_gnn_a_r': _L1_gnn_in['a_r'], 'L2_gnn_W': _L2_gnn_in['W'], 'L2_gnn_b': _L2_gnn_in['b'], 'L3_gnn_weight': _L3_gnn_in['weight'], 'L3_gnn_attn_l': _L3_gnn_in['attn_l'], 'L3_gnn_attn_r': _L3_gnn_in['attn_r']}

def reference(x, src, dst, edge_weight, node_vec, L0_gnn_kernel, L0_gnn_bias, L1_gnn_W, L1_gnn_a_l, L1_gnn_a_r, L2_gnn_W, L2_gnn_b, L3_gnn_weight, L3_gnn_attn_l, L3_gnn_attn_r):
    import jax
    import jax.numpy as jnp

    def _L0_gnn_ref(x, edge_row, edge_col, edge_vals, kernel, bias):
        import jax, jax.numpy as jnp
        import numpy as np
        N = 3125
        E = 100000
        F = 256
        C = 256
        h = x @ kernel
        msgs = edge_vals[:, None] * h[edge_col]
        agg = jax.ops.segment_sum(msgs, edge_row, num_segments=N)
        return jax.nn.relu(agg + bias)

    def _L1_gnn_ref(x, edge, W, a_l, a_r):
        import jax, jax.numpy as jnp
        import numpy as np
        N = 50000
        E = 25000
        IN_F = 256
        OUT_F = 64
        NHEAD = 4
        ALPHA = 0.2

        def _gat_forward(x, W, a_l, a_r, edge):
            n = x.shape[0]
            row, col = (edge[0], edge[1])
            h = (x @ W).reshape(n, NHEAD, OUT_F)
            hl = jnp.sum(a_l * h, axis=-1)
            hr = jnp.sum(a_r * h, axis=-1)
            e = jax.nn.leaky_relu(hl[row] + hr[col], negative_slope=ALPHA)
            e_max = jax.ops.segment_max(e, row, num_segments=n)
            e_max = jnp.where(jnp.isfinite(e_max), e_max, 0.0)
            ee = jnp.exp(e - e_max[row])
            denom = jax.ops.segment_sum(ee, row, num_segments=n)
            att = ee / denom[row]
            msg = att[:, :, None] * h[col]
            out_h = jax.ops.segment_sum(msg, row, num_segments=n)
            return out_h.reshape(n, NHEAD * OUT_F)
        return _gat_forward(x, W, a_l, a_r, edge)

    def _L2_gnn_ref(x, hyperedge_index, hyperedge_weight, W, b):
        import jax, jax.numpy as jnp
        import numpy as np
        NUM_NODES = 50000
        NUM_EDGES = 50000
        NNZ = 15625
        D_IN = 256
        D_OUT = 256
        num_nodes = x.shape[0]
        num_edges = hyperedge_weight.shape[0]
        node_idx = hyperedge_index[0]
        edge_idx = hyperedge_index[1]
        xl = x @ W
        D = jax.ops.segment_sum(hyperedge_weight[edge_idx], node_idx, num_segments=num_nodes)
        Dinv = jnp.where(D > 0, 1.0 / D, 0.0)
        Bc = jax.ops.segment_sum(jnp.ones((node_idx.shape[0],), dtype=xl.dtype), edge_idx, num_segments=num_edges)
        Binv = jnp.where(Bc > 0, 1.0 / Bc, 0.0)
        e_feat = jax.ops.segment_sum(Binv[edge_idx][:, None] * xl[node_idx], edge_idx, num_segments=num_edges)
        out = jax.ops.segment_sum(Dinv[node_idx][:, None] * e_feat[edge_idx], node_idx, num_segments=num_nodes)
        return out + b

    def _L3_gnn_ref(x, edge_index, weight, attn_l, attn_r):
        import jax, jax.numpy as jnp
        import numpy as np
        N, IN_CH, HEADS, OUT_CH, E = (50000, 256, 4, 64, 25000)
        heads, out_ch = attn_l.shape
        n = x.shape[0]
        xt = jnp.matmul(x, weight).reshape(-1, heads, out_ch)
        row, col = (edge_index[0], edge_index[1])
        alpha_l = jnp.einsum('ehd,hd->eh', xt[row], attn_l)
        alpha_r = jnp.einsum('ehd,hd->eh', xt[col], attn_r)
        alpha = jax.nn.softmax(jax.nn.leaky_relu(alpha_l + alpha_r, 0.01), axis=1)
        tmp = jnp.einsum('nh,nhd->nd', alpha[:n], xt[col[:n]])
        out = jnp.broadcast_to(tmp[:, None, :], (n, heads, out_ch))
        return out.reshape(n, heads * out_ch)
    edge_index = jnp.stack([src, dst])
    x = _layernorm(x + _L0_gnn_ref(x, src, dst, edge_weight, L0_gnn_kernel, L0_gnn_bias), axis=-1)
    x = _layernorm(x + _L1_gnn_ref(x, edge_index, L1_gnn_W, L1_gnn_a_l, L1_gnn_a_r), axis=-1)
    x = _layernorm(x + _L2_gnn_ref(x, edge_index, node_vec, L2_gnn_W, L2_gnn_b), axis=-1)
    x = _layernorm(x + _L3_gnn_ref(x, edge_index, L3_gnn_weight, L3_gnn_attn_l, L3_gnn_attn_r), axis=-1)
    return x

_drawn_inputs = setup_inputs


def setup_inputs(seed=0):
    import zlib

    import numpy as np

    out = dict(_drawn_inputs(seed))
    spreads = {'L0_gnn_bias': (0.0, 0.1)}
    factors = {'L2_gnn_b': 5.197}
    for name, (base, spread) in spreads.items():
        noise = np.random.default_rng([zlib.crc32(name.encode()), seed]).standard_normal(out[name].shape)
        drawn = base * np.exp(spread * noise) if base else spread * noise
        out[name] = jnp.asarray(drawn.astype(out[name].dtype))
    for name, factor in factors.items():
        out[name] = (out[name] * factor).astype(out[name].dtype)
    return out
```

```python
from contextlib import ExitStack

import numpy as np

import concourse.bass as bass
from concourse import mybir

F32 = mybir.dt.float32
BF16 = mybir.dt.bfloat16
I32 = mybir.dt.int32
ALU = mybir.AluOpType
ACT = mybir.ActivationFunctionType
AX = mybir.AxisListType

N, E, F = 3125, 50000, 256
TILES, P = 25, 125
HEADS, HD = 4, 64
HX = HD + 1
FX = HEADS * HX
CH = 18
WIN = CH * 128
RANKS = 128
PAY = 5
GEN = E // P
HALF = [12, 13]
START = [0, 12]
GROUPS = [(0, 3), (3, 3), (6, 3), (9, 3), (12, 3), (15, 3), (18, 3), (21, 4)]
CREDIT = 8
THIRDS = [(0, 9), (9, 9), (18, 7)]
MAGIC = 12582912.0
EPS = 1e-5
SPREAD = 60.0


class Count:

    def __init__(self, base=0):
        self.base, self.k = base, 0

    def one(self):
        self.k += 1
        return 1

    def now(self):
        return self.base + self.k


def at(i):
    return bass.ds(i, 1)


def tensors(nc, ctx):
    def sb(name, shape, dt=F32):
        return ctx.enter_context(nc.sbuf_tensor(name, shape, dt))

    m = {}
    m["x"] = sb("x_sb", [P, TILES, F])
    m["hx"] = sb("hx", [P, TILES, FX])
    m["hs"] = sb("hs", [P, 3, TILES, FX], BF16)
    m["w"] = sb("w_sb", [128, 4, 2, F])
    m["arena"] = sb("arena", [128, 10400])
    m["table"] = sb("table", [128, 3, TILES, TILES])
    m["nv"] = sb("nv_sb", [P, TILES])
    m["ident"] = sb("ident", [128, 128])
    m["identb"] = sb("identb", [128, 128], BF16)
    m["ones"] = sb("ones", [128, 128])
    m["earlier"] = sb("earlier", [128, 128], BF16)
    m["one_up"] = sb("one_up", [128, 128])
    m["row"] = sb("row", [128, 1])
    m["starts"] = sb("starts", [1, 32], I32)
    m["flags"] = sb("flags", [1, 2], I32)
    m["bias0"] = sb("bias0", [P, F])
    m["bias2"] = sb("bias2", [P, F])
    m["attn"] = sb("attn", [P, 4, F])
    m["hl"] = sb("hl", [P, TILES, HEADS])
    m["hr"] = sb("hr", [P, TILES, HEADS])
    m["logit"] = sb("logit", [P, TILES, 3, 12], BF16)
    return m


def load_and_starts(nc, m, d):
    with ExitStack() as ctx:
        loaded = ctx.enter_context(nc.semaphore("loaded"))
        dst_in = ctx.enter_context(nc.semaphore("dst_in"))
        iotas = ctx.enter_context(nc.semaphore("iotas"))
        made = ctx.enter_context(nc.semaphore("made"))
        summed = ctx.enter_context(nc.semaphore("summed"))
        dst_i = ctx.enter_context(nc.sbuf_tensor("dst_i", [P, GEN], I32))
        dst_f = m["arena"][0:P, 0:GEN]
        less = m["arena"][0:P, GEN:2 * GEN]
        below = m["arena"][0:P, 2 * GEN:2 * GEN + TILES]
        grid = ctx.enter_context(nc.sbuf_tensor("grid", [128, 128], I32))
        rowi = ctx.enter_context(nc.sbuf_tensor("rowi", [128, 1], I32))
        first = ctx.enter_context(nc.sbuf_tensor("first", [1, TILES], F32))
        total = ctx.enter_context(nc.psum_tensor("total", [1, TILES], F32))
        block = ctx.enter_context(nc.Block())
        loads = 7 + 4

        @block.sync
        def _(sync):
            sync.dma_start(dst_i[:, :], d["dst"].rearrange("(p c) -> p c", c=GEN)).then_inc(dst_in, 16)
            sync.dma_start(m["x"][:, :, :], d["x"].rearrange("(t p) f -> p t f", p=P)).then_inc(loaded, 16)
            for n, name in enumerate(("w0", "w1", "w2", "w3")):
                sync.dma_start(m["w"][:, n, :, :], d[name].rearrange("(c k) n -> k c n", k=128)).then_inc(loaded, 16)
            sync.dma_start(m["bias0"][:, :], d["bias0"].partition_broadcast(P)).then_inc(loaded, 16)
            sync.dma_start(m["bias2"][:, :], d["bias2"].partition_broadcast(P)).then_inc(loaded, 16)
            for n, name in enumerate(("al1", "ar1", "al3", "ar3")):
                sync.dma_start(m["attn"][:, n, :], d[name].partition_broadcast(P)).then_inc(loaded, 16)
            with nc.allow_non_contiguous_dma(reason="12.5 KB, once"):
                sync.dma_start(m["nv"][:, :], d["nv"].rearrange("(t p) -> p t", p=P)).then_inc(loaded, 16)
            sync.wait_ge(loaded, 16 * 12)

        @block.gpsimd
        def _(pool):
            pool.iota(grid[:, :], [[1, 128]], base=1, channel_multiplier=0).then_inc(iotas, 1)
            pool.iota(rowi[:, :], [[1, 1]], base=1, channel_multiplier=1).then_inc(iotas, 1)
            pool.memset(m["ones"][:, :], 1.0).then_inc(iotas, 1)

        @block.vector
        def _(vec):
            vec.wait_ge(iotas, 3)
            vec.tensor_copy(m["one_up"][:, :], grid[:, :]).then_inc(made, 1)
            vec.tensor_copy(m["row"][:, :], rowi[:, :]).then_inc(made, 1)
            vec.wait_ge(made, 2)
            vec.tensor_scalar(m["ident"][:, :], m["one_up"][:, :], m["row"][:, :], None, ALU.is_equal).then_inc(made, 1)
            vec.tensor_scalar(m["identb"][:, :], m["one_up"][:, :], m["row"][:, :], None, ALU.is_equal).then_inc(made, 1)
            vec.tensor_scalar(m["earlier"][:, :], m["one_up"][:, :], m["row"][:, :], None, ALU.is_gt).then_inc(made, 1)
            vec.wait_ge(dst_in, 16)
            vec.tensor_copy(dst_f, dst_i[:, :]).then_inc(made, 1)
            for j in range(TILES):
                vec.wait_ge(made, 6 + j)
                vec.tensor_scalar(less, dst_f, float(P * j), None, ALU.is_lt, ALU.add,
                                  accum_out=below[:, j:j + 1]).then_inc(made, 1)
            vec.wait_ge(summed, 1)
            vec.tensor_scalar(first[:, :], total[:, :], float(E - WIN), None, ALU.min).then_inc(made, 1)
            vec.wait_ge(made, 7 + TILES)
            vec.tensor_copy(m["starts"][:, 0:TILES], first[:, :]).then_inc(made, 1)

        @block.tensor
        def _(pe):
            pe.wait_ge(made, 6 + TILES)
            pe.matmul(total[:, :], m["ones"][0:P, 0:1], below, start=True, stop=True).then_inc(summed, 1)


def in_pairs(eng, body):
    with eng.Fori(0, TILES // 2) as pair:
        body(2 * pair, 0, True)
        body(2 * pair + 1, 1, True)
    body(TILES - 1, 0, False)


def build_table(nc, m, d):
    with ExitStack() as ctx:
        def sem(name):
            return ctx.enter_context(nc.semaphore(name))

        def sb(name, shape, dt=F32):
            return ctx.enter_context(nc.sbuf_tensor(name, shape, dt))

        win_in = sem("win_in")
        iotas = sem("iotas")
        calc = sem("calc")
        step = sem("step")
        tile_hot = sem("tile_hot")
        counts_ready = sem("counts_ready")
        base_ready = sem("base_ready")
        rank_hot = sem("rank_hot")
        pay_ready = sem("pay_ready")
        moved = sem("moved")
        kept = sem("kept")
        turned = sem("turned")
        rows_out = sem("rows_out")
        stored = sem("stored")
        src_i = sb("src_w", [128, TILES, CH], I32)
        dst_i = sb("dst_w", [128, TILES, CH], I32)
        starts_i = sb("starts_i", [128, TILES], I32)
        starts_f = sb("starts_f", [128, TILES])
        values = sb("values", [128, PAY, TILES, CH], BF16)
        weight = sb("weight", [128, TILES, CH])
        tile_of = sb("tile_of", [128, TILES, CH])
        t1, t2, t3 = (sb(f"t{n}", [128, TILES, CH]) for n in (1, 2, 3))
        raw = sb("raw", [128, PAY, TILES, TILES], BF16)
        placed = sb("placed", [128, 1])
        all_in = sb("all_in", [1, 1])
        arena, taken = m["arena"], [0]

        def take(n, dt=F32):
            words = n if dt == F32 else n // 2
            taken[0] += words
            part = arena[:, taken[0] - words:taken[0]]
            return part if dt == F32 else part.bitcast(dt)

        def by_tile(t):
            return t.rearrange("p (a c) -> p a c", c=CH)

        hot = [take(TILES * CH) for _ in range(2)]
        running, keep, rank_of = take(TILES * CH), take(TILES * CH), take(TILES * CH)
        rank = take(CH)
        counts = take(32, BF16)
        ranks = [take(CH * RANKS, BF16).rearrange("p (c r) -> p c r", r=RANKS) for _ in range(2)]
        pay = [take(CH * PAY * TILES, BF16).rearrange("p (c k a) -> p c k a", c=CH, k=PAY) for _ in range(2)]
        scratch = take(TILES * TILES)
        rows = take(10 * RANKS, BF16).rearrange("p (k r) -> p k r", r=RANKS)
        base = ctx.enter_context(nc.psum_tensor("base", [128, 512], F32))
        out = [ctx.enter_context(nc.psum_tensor(f"buckets{i}", [128, 512], F32)) for i in range(2)]
        turn = ctx.enter_context(nc.psum_tensor("turn", [128, 2, 1024], BF16))
        block = ctx.enter_context(nc.Block())

        @block.sync
        def _(sync):
            with sync.Fori(0, TILES) as j:
                start = sync.value_load(m["starts"][0:1, at(j)], min_val=0, max_val=E - WIN)
                for tile, name in ((src_i, "src"), (dst_i, "dst"), (weight, "ew")):
                    sync.dma_start(tile[:, at(j), :],
                                   d[name][bass.ds(start, WIN)].rearrange("(p o c) -> p o c", p=128, o=1)
                                   ).then_inc(win_in, 16)
            sync.wait_ge(rows_out, 2)
            for k in range(2):
                sync.dma_start(d["rows"][k].rearrange("(c p) r -> p c r", p=P),
                               rows[0:P, 5 * k:5 * k + 5, :]).then_inc(stored, 16)
            sync.wait_ge(stored, 32)

        @block.gpsimd
        def _(pool):
            pool.iota(starts_i[:, :], [[P, TILES]], base=-1, channel_multiplier=0).then_inc(iotas, 1)
            pool.memset(keep, 1.0).then_inc(iotas, 1)
            pool.wait_ge(iotas, 2)
            pool.memset(by_tile(keep)[:, :, 0:1], 0.0).then_inc(iotas, 1)
            pool.wait_ge(calc, 14)

            def payload(j, slot, more):
                pool.wait_ge(tile_hot, j + 1)
                pool.wait_ge(moved, CREDIT + j - 1)
                pool.tensor_tensor(
                    pay[slot],
                    by_tile(hot[slot]).rearrange("p a (c o) -> p c o a", o=1).to_broadcast([128, CH, PAY, TILES]),
                    values[:, :, at(j), :].rearrange("p k o (c b) -> p (o c) k b", b=1).to_broadcast(
                        [128, CH, PAY, TILES]), ALU.mult).then_inc(pay_ready, 1)

            in_pairs(pool, payload)

        @block.vector
        def _(vec):
            n = Count()
            vec.wait_ge(win_in, 16 * 3 * TILES)
            vec.wait_ge(iotas, 3)
            vec.tensor_copy(t1[:, :, :], src_i[:, :, :]).then_inc(calc, n.one())
            vec.tensor_copy(t2[:, :, :], dst_i[:, :, :]).then_inc(calc, n.one())
            vec.tensor_copy(starts_f[:, :], starts_i[:, :]).then_inc(calc, n.one())
            vec.tensor_copy(values[:, 2, :, :], weight[:, :, :]).then_inc(calc, n.one())
            vec.wait_ge(calc, n.now())
            vec.tensor_tensor(t2[:, :, :], t2[:, :, :],
                              starts_f[:, :].rearrange("p (j o) -> p j o", o=1).to_broadcast([128, TILES, CH]),
                              ALU.subtract).then_inc(calc, n.one())
            vec.tensor_scalar(t3[:, :, :], t1[:, :, :], 1.0 / P, 0.5 / P - 0.5, ALU.mult, ALU.add
                              ).then_inc(calc, n.one())
            vec.tensor_tensor(weight[:, :, :], weight[:, :, :], values[:, 2, :, :], ALU.subtract
                              ).then_inc(calc, n.one())
            vec.wait_ge(calc, n.now())
            vec.tensor_scalar(t3[:, :, :], t3[:, :, :], MAGIC, None, ALU.add).then_inc(calc, n.one())
            vec.tensor_copy(values[:, 1, :, :], t2[:, :, :]).then_inc(calc, n.one())
            vec.tensor_copy(values[:, 3, :, :], weight[:, :, :]).then_inc(calc, n.one())
            vec.wait_ge(calc, n.now())
            vec.tensor_scalar(t3[:, :, :], t3[:, :, :], MAGIC, None, ALU.subtract).then_inc(calc, n.one())
            vec.tensor_tensor(values[:, 4, :, :], weight[:, :, :], values[:, 3, :, :], ALU.subtract
                              ).then_inc(calc, n.one())
            vec.wait_ge(calc, n.now())
            vec.scalar_tensor_tensor(t1[:, :, :], t3[:, :, :], -float(P), t1[:, :, :], ALU.mult, ALU.add
                                     ).then_inc(calc, n.one())
            vec.wait_ge(calc, n.now())
            vec.tensor_scalar(values[:, 0, :, :], t1[:, :, :], 1.0, None, ALU.add).then_inc(calc, n.one())
            vec.wait_ge(calc, n.now())
            vec.tensor_scalar(t1[:, :, :], t2[:, :, :], 1.0, None, ALU.is_ge).then_inc(calc, n.one())
            vec.wait_ge(calc, n.now())
            vec.scalar_tensor_tensor(t1[:, :, :], t2[:, :, :], float(P), t1[:, :, :], ALU.is_le, ALU.mult
                                     ).then_inc(calc, n.one())
            vec.wait_ge(calc, n.now())
            vec.scalar_tensor_tensor(tile_of[:, :, :], t3[:, :, :], 1.0, t1[:, :, :], ALU.add, ALU.mult
                                     ).then_inc(calc, n.one())
            vec.wait_ge(calc, n.now())
            vec.sem_inc(moved, CREDIT)
            vec.sem_inc(kept, CREDIT)

            def sort_tile(j, slot, more):
                s = Count(4 * j)
                onehot = by_tile(hot[slot])
                vec.wait_ge(pay_ready, CREDIT + j - 1)
                vec.tensor_tensor(
                    onehot, tile_of[:, at(j), :].to_broadcast([128, TILES, CH]),
                    m["one_up"][:, 0:TILES].rearrange("p (a o) -> p a o", o=1).to_broadcast([128, TILES, CH]),
                    ALU.is_equal).then_inc(tile_hot, 1)
                vec.wait_ge(tile_hot, j + 1)
                vec.tensor_tensor_scan(running, keep, hot[slot], 0.0, ALU.mult, ALU.add).then_inc(step, s.one())
                vec.wait_ge(step, s.now())
                vec.tensor_copy(counts[:, 0:TILES], by_tile(running)[:, :, CH - 1]).then_inc(counts_ready, 1)
                vec.wait_ge(base_ready, j + 1)
                vec.tensor_tensor(
                    by_tile(rank_of), by_tile(running),
                    base[:, 0:TILES].rearrange("p (a o) -> p a o", o=1).to_broadcast([128, TILES, CH]), ALU.add
                    ).then_inc(step, s.one())
                vec.wait_ge(step, s.now())
                vec.tensor_tensor(rank_of, rank_of, hot[slot], ALU.mult).then_inc(step, s.one())
                vec.wait_ge(step, s.now())
                vec.tensor_reduce(rank, by_tile(rank_of).rearrange("p a c -> p c a"), AX.X, ALU.add
                                  ).then_inc(step, s.one())
                vec.wait_ge(step, s.now())
                vec.wait_ge(moved, CREDIT + j - 1)
                vec.tensor_tensor(
                    ranks[slot], rank.rearrange("p (c o) -> p c o", o=1).to_broadcast([128, CH, RANKS]),
                    m["one_up"][:, :].rearrange("p (o r) -> p o r", o=1).to_broadcast([128, CH, RANKS]),
                    ALU.is_equal).then_inc(rank_hot, 1)

            vec.sem_inc(pay_ready, CREDIT)
            in_pairs(vec, sort_tile)

            vec.wait_ge(kept, CREDIT + TILES)
            vec.tensor_copy(m["table"][:, 0:2, :, :], raw[:, 0:2, :, :]).then_inc(calc, n.one())
            vec.tensor_tensor(m["table"][:, 2, :, :], raw[:, 3, :, :], raw[:, 4, :, :], ALU.add
                              ).then_inc(calc, n.one())
            vec.wait_ge(calc, n.now())
            vec.tensor_tensor(m["table"][:, 2, :, :], m["table"][:, 2, :, :], raw[:, 2, :, :], ALU.add
                              ).then_inc(calc, n.one())
            vec.tensor_scalar(scratch, m["table"][:, 1, :, :].rearrange("p a j -> p (a j)"), 0.0, None,
                              ALU.is_gt, ALU.add, accum_out=placed[:, :]).then_inc(calc, n.one())
            vec.wait_ge(base_ready, TILES + 1)
            vec.tensor_scalar(all_in[:, :], base[0:1, 0:1], float(E), None, ALU.is_equal).then_inc(calc, n.one())
            vec.wait_ge(calc, n.now())
            vec.tensor_copy(m["flags"][:, 0:1], all_in[:, :]).then_inc(calc, n.one())

        @block.tensor
        def _(pe):
            def move(j, slot, more):
                pe.wait_ge(counts_ready, j + 1)
                pe.matmul(base[:, 0:TILES], m["earlier"][:, :], counts[:, 0:TILES], start=True, stop=True
                          ).then_inc(base_ready, 1)
                pe.wait_ge(rank_hot, j + 1)
                pe.wait_ge(pay_ready, CREDIT + j + 1)
                pe.wait_ge(kept, CREDIT + j - 1)
                for c in range(CH):
                    last = pe.matmul(out[slot][:, 0:PAY * TILES], ranks[slot][:, c, :],
                                     pay[slot][:, c, :, :].rearrange("p k a -> p (k a)"),
                                     start=c == 0, stop=c == CH - 1)
                last.then_inc(moved, 1)

            in_pairs(pe, move)
            pe.wait_ge(calc, 21)
            pe.matmul(base[0:1, 0:1], m["ones"][:, 0:1], placed[:, :], start=True, stop=True).then_inc(base_ready, 1)
            for k in range(2):
                for c in range(5):
                    last = pe.transpose(turn[0:P, k, c * RANKS:(c + 1) * RANKS],
                                        raw[:, k, 5 * c:5 * c + 5, :].rearrange("p a j -> p (a j)"),
                                        m["identb"][:, :])
                last.then_inc(turned, 1)

        @block.scalar
        def _(act):
            def keep_tile(j, slot, more):
                act.wait_ge(moved, CREDIT + j + 1)
                act.copy(raw[:, :, :, at(j)].rearrange("p k a o -> p k (a o)"),
                         out[slot][:, 0:PAY * TILES].rearrange("p (k a) -> p k a", k=PAY)).then_inc(kept, 1)

            in_pairs(act, keep_tile)
            for k in range(2):
                act.wait_ge(turned, k + 1)
                act.copy(rows[0:P, 5 * k:5 * k + 5, :],
                         turn[0:P, k, 0:5 * RANKS].rearrange("p (c r) -> p c r", r=RANKS)).then_inc(rows_out, 1)


def project(nc, m, weight, layer, split, attn=None):
    with ExitStack() as ctx:
        def sem(name):
            return ctx.enter_context(nc.semaphore(f"{name}_p{layer}"))

        def sb(name, shape, dt=F32):
            return [ctx.enter_context(nc.sbuf_tensor(f"{name}_p{layer}_{i}", shape, dt)) for i in range(2)]

        staged = sem("staged")
        turned = sem("turned")
        turned_kept = sem("turned_kept")
        product = sem("product")
        copied = sem("copied")
        step = sem("step")
        filled = sem("filled")
        xs, xt, rest = sb("xs", [P, F]), sb("xt", [128, 2, P]), sb("rest", [P, F])
        by_l, by_r = sb("by_l", [P, F]), sb("by_r", [P, F])
        pt = [ctx.enter_context(nc.psum_tensor(f"pt{layer}_{i}", [128, 512], F32)) for i in range(2)]
        ph = [ctx.enter_context(nc.psum_tensor(f"ph{layer}_{i}", [P, 512], F32)) for i in range(2)]
        hxv = m["hx"][:, :, :].rearrange("p t (h e) -> p t h e", e=HX)
        hsv = m["hs"][:, :, :, :].rearrange("p s t (h e) -> p s t h e", e=HX)
        copies = 2 if split else 1
        steps = 3 * bool(split) + 4 * (attn is not None)

        def heads(t):
            return t.rearrange("p (h d) -> p h d", d=HD)

        def row(t, j):
            return t[:, at(j), :, 0:HD].rearrange("p o h d -> p (o h) d")

        block = ctx.enter_context(nc.Block())

        @block.gpsimd
        def _(pool):
            if split:
                pool.memset(hxv[:, :, :, HD], 1.0).then_inc(filled, 1)
                pool.memset(hsv[:, 0, :, :, HD], 1.0).then_inc(filled, 1)
                pool.memset(hsv[:, 1, :, :, HD], 0.0).then_inc(filled, 1)
                pool.memset(hsv[:, 2, :, :, HD], 0.0).then_inc(filled, 1)

            def tile(j, slot, more):
                pool.wait_ge(turned, CREDIT + j - 1)
                pool.tensor_copy(xs[slot][:, :], m["x"][:, at(j), :].rearrange("p o f -> p (o f)")
                                 ).then_inc(staged, 1)

            pool.sem_inc(turned_kept, CREDIT)
            in_pairs(pool, tile)

        @block.tensor
        def _(pe):
            def turn(j, slot):
                pe.wait_ge(staged, j + 1)
                pe.wait_ge(turned_kept, CREDIT + j - 1)
                for c in range(2):
                    last = pe.transpose(pt[slot][:, c * 128:c * 128 + P], xs[slot][:, c * 128:(c + 1) * 128],
                                        m["ident"][0:P, 0:P])
                last.then_inc(turned, 1)

            def tile(j, slot, more):
                if more:
                    turn(j + 1, 1 - slot)
                pe.wait_ge(turned_kept, CREDIT + j + 1)
                pe.wait_ge(copied, copies * j + CREDIT - copies)
                for c in range(2):
                    last = pe.matmul(ph[slot][:, 0:F], xt[slot][:, c, :], m["w"][:, weight, c, :],
                                     start=c == 0, stop=c == 1)
                last.then_inc(product, 1)

            pe.sem_inc(turned, CREDIT)
            turn(0, 0)
            in_pairs(pe, tile)

        @block.scalar
        def _(act):
            def keep(j, slot):
                act.wait_ge(turned, CREDIT + j + 1)
                act.wait_ge(product, CREDIT + j - 1)
                act.copy(xt[slot][:, :, :], pt[slot][:, 0:256].rearrange("p (c n) -> p c n", c=2)[:, :, 0:P]
                         ).then_inc(turned_kept, 1)

            def tile(j, slot, more):
                if more:
                    keep(j + 1, 1 - slot)
                act.wait_ge(product, CREDIT + j + 1)
                if split:
                    act.copy(row(hsv[:, 0], j), heads(ph[slot][:, 0:F])).then_inc(copied, 1)
                act.copy(row(hxv, j), heads(ph[slot][:, 0:F])).then_inc(copied, 1)

            act.sem_inc(product, CREDIT)
            keep(0, 0)
            in_pairs(act, tile)

        @block.vector
        def _(vec):
            def tile(j, slot, more):
                s = Count(steps * j)
                h = row(hxv, j)
                vec.wait_ge(copied, CREDIT + copies * (j + 1))
                if attn is not None:
                    for n, by in enumerate((by_l, by_r)):
                        vec.tensor_tensor(heads(by[slot][:, :]), h, heads(m["attn"][:, attn + n, :]), ALU.mult
                                          ).then_inc(step, s.one())
                if split:
                    vec.tensor_tensor(heads(rest[slot][:, :]), h, row(hsv[:, 0], j), ALU.subtract
                                      ).then_inc(step, s.one())
                vec.wait_ge(step, s.now())
                if split:
                    vec.tensor_copy(row(hsv[:, 1], j), heads(rest[slot][:, :])).then_inc(step, s.one())
                if attn is not None:
                    for by, into in ((by_l, "hl"), (by_r, "hr")):
                        vec.tensor_reduce(m[into][:, at(j), :].rearrange("p o h -> p (o h)"),
                                          heads(by[slot][:, :]), AX.X, ALU.add).then_inc(step, s.one())
                if split:
                    vec.wait_ge(step, s.now())
                    vec.tensor_tensor(row(hsv[:, 2], j), heads(rest[slot][:, :]), row(hsv[:, 1], j), ALU.subtract
                                      ).then_inc(step, s.one())

            vec.sem_inc(copied, CREDIT)
            if steps:
                in_pairs(vec, tile)


def attention_inputs(nc, m):
    with ExitStack() as ctx:
        def sb(name, shape, dt=F32):
            return ctx.enter_context(nc.sbuf_tensor(name, shape, dt))

        step = ctx.enter_context(nc.semaphore("step_a"))
        done = ctx.enter_context(nc.semaphore("done_a"))
        ends = sb("ends", [P, 8])
        top = sb("top", [8, 1])
        spread_out = sb("spread_out", [8, 8])
        of_all = sb("of_all", [P, 8])
        cat = sb("cat", [P, TILES, 12])
        rest = sb("rest_a", [P, TILES, 12])
        small = sb("small", [1, 4])
        flag = sb("flag_f", [1, 2])
        pa = ctx.enter_context(nc.psum_tensor("pa", [128, 512], F32))
        pb = ctx.enter_context(nc.psum_tensor("pb", [128, 512], F32))
        block = ctx.enter_context(nc.Block())

        @block.tensor
        def _(pe):
            pe.wait_ge(step, 3)
            pe.transpose(pa[0:8, 0:P], ends[:, :], m["ident"][0:P, 0:P]).then_inc(done, 1)
            pe.wait_ge(step, 7)
            pe.matmul(pb[0:P, 0:8], m["ones"][0:8, 0:P], spread_out[:, :], start=True, stop=True).then_inc(done, 1)

        @block.vector
        def _(vec):
            n = Count()
            by_head = m["hr"][:, :, :].rearrange("p t h -> p h t")
            logits = cat[:, :, 4:8]
            vec.tensor_reduce(ends[:, 0:4], by_head, AX.X, ALU.max).then_inc(step, n.one())
            vec.tensor_reduce(ends[:, 4:8], by_head, AX.X, ALU.min).then_inc(step, n.one())
            vec.wait_ge(step, n.now())
            vec.tensor_scalar(ends[:, 4:8], ends[:, 4:8], -1.0, None, ALU.mult).then_inc(step, n.one())
            vec.tensor_copy(cat[:, :, 0:4], m["hl"][:, :, :]).then_inc(step, n.one())
            vec.tensor_copy(cat[:, :, 8:12], m["hr"][:, :, :]).then_inc(step, n.one())
            vec.wait_ge(done, 1)
            vec.tensor_reduce(top[:, :], pa[0:8, 0:P], AX.X, ALU.max).then_inc(step, n.one())
            vec.wait_ge(step, n.now())
            vec.tensor_scalar(spread_out[:, :], m["ident"][0:8, 0:8], top[:, :], None, ALU.mult
                              ).then_inc(step, n.one())
            vec.wait_ge(done, 2)
            vec.tensor_copy(of_all[:, :], pb[0:P, 0:8]).then_inc(step, n.one())
            vec.wait_ge(step, n.now())
            vec.tensor_tensor(logits, m["hl"][:, :, :],
                              of_all[:, 0:4].rearrange("p (o h) -> p o h", o=1).to_broadcast([P, TILES, HEADS]),
                              ALU.add).then_inc(step, n.one())
            vec.tensor_tensor(small[:, :], of_all[0:1, 0:4], of_all[0:1, 4:8], ALU.add).then_inc(step, n.one())
            vec.tensor_copy(flag[:, 0:1], m["flags"][:, 0:1]).then_inc(step, n.one())
            vec.wait_ge(step, n.now())
            vec.scalar_tensor_tensor(logits, logits, 0.2, logits, ALU.mult, ALU.max).then_inc(step, n.one())
            vec.tensor_reduce(flag[:, 1:2], small[:, :], AX.X, ALU.max).then_inc(step, n.one())
            vec.wait_ge(step, n.now())
            vec.tensor_copy(m["logit"][:, :, 0, :], cat[:, :, :]).then_inc(step, n.one())
            vec.scalar_tensor_tensor(flag[:, 1:2], flag[:, 1:2], SPREAD, flag[:, 0:1], ALU.is_le, ALU.mult
                                     ).then_inc(step, n.one())
            vec.wait_ge(step, n.now())
            vec.tensor_tensor(rest[:, :, :], cat[:, :, :], m["logit"][:, :, 0, :], ALU.subtract
                              ).then_inc(step, n.one())
            vec.tensor_copy(m["flags"][:, 1:2], flag[:, 1:2]).then_inc(step, n.one())
            vec.wait_ge(step, n.now())
            vec.tensor_copy(m["logit"][:, :, 1, :], rest[:, :, :]).then_inc(step, n.one())
            vec.wait_ge(step, n.now())
            vec.tensor_tensor(m["logit"][:, :, 2, :], rest[:, :, :], m["logit"][:, :, 1, :], ALU.subtract
                              ).then_inc(step, n.one())


def split_edges(nc, m):
    with ExitStack() as ctx:
        filled = ctx.enter_context(nc.semaphore("filled_s"))
        firsts = ctx.enter_context(nc.semaphore("firsts"))
        seconds = ctx.enter_context(nc.semaphore("seconds"))
        rests = ctx.enter_context(nc.semaphore("rests"))
        thirds = ctx.enter_context(nc.semaphore("thirds"))
        block = ctx.enter_context(nc.Block())
        rest = m["arena"][0:P, 0:TILES * FX].rearrange("p (t e) -> p t e", e=FX)
        parts = [slice(5 * g, 5 * g + 5) for g in range(5)]

        @block.gpsimd
        def _(pool):
            pool.tensor_copy(m["hx"][:, :, :].rearrange("p t (h e) -> p t h e", e=HX)[:, :, :, HD],
                             m["nv"][:, :].rearrange("p (t o) -> p t o", o=1).to_broadcast([P, TILES, HEADS])
                             ).then_inc(filled, 1)

        @block.scalar
        def _(act):
            act.wait_ge(filled, 1)
            for g, part in enumerate(parts):
                act.copy(m["hs"][:, 0, part, :], m["hx"][:, part, :]).then_inc(firsts, 1)
                act.wait_ge(rests, g + 1)
                act.copy(m["hs"][:, 1, part, :], rest[:, part, :]).then_inc(seconds, 1)

        @block.vector
        def _(vec):
            vec.wait_ge(filled, 1)
            for g, part in enumerate(parts):
                vec.wait_ge(firsts, g + 1)
                vec.tensor_tensor(rest[:, part, :], m["hx"][:, part, :], m["hs"][:, 0, part, :], ALU.subtract
                                  ).then_inc(rests, 1)
                vec.wait_ge(seconds, g + 1)
                vec.tensor_tensor(m["hs"][:, 2, part, :], rest[:, part, :], m["hs"][:, 1, part, :], ALU.subtract
                                  ).then_inc(thirds, 1)


class Finish:

    STEPS = {0: 6, 1: 8, 2: 2, 3: 12}

    def __init__(self, nc, ctx, m, kind, psum_sums):
        def sb(name, shape):
            return ctx.enter_context(nc.sbuf_tensor(f"{name}_f{kind}", shape, F32))

        self.m, self.kind, self.sums = m, kind, psum_sums
        self.step = ctx.enter_context(nc.semaphore(f"step_f{kind}"))
        self.variance = ctx.enter_context(nc.semaphore(f"variance_f{kind}"))
        self.deviation = ctx.enter_context(nc.semaphore(f"deviation_f{kind}"))
        self.sums_used = ctx.enter_context(nc.semaphore(f"sums_used_f{kind}"))
        self.new, self.out = sb("new", [P, F]), sb("out", [P, F])
        self.small, self.stats, self.mean = sb("small", [P, 8]), sb("stats", [P, 6]), sb("mean", [P, 2])
        self.dev, self.inv = sb("dev", [P, 1]), sb("inv", [P, 1])

    def sqrt(self, act, j):
        act.wait_ge(self.variance, j + 1)
        act.activation(self.dev[:, :], self.mean[:, 1:2], ACT.Sqrt).then_inc(self.deviation, 1)

    def normalize(self, vec, s, j):
        m, step = self.m, self.step
        vec.bn_stats(self.stats[:, :], self.new[:, :]).then_inc(step, s.one())
        vec.drain()
        vec.bn_aggr(self.mean[:, :], self.stats[:, :]).then_inc(step, s.one())
        vec.wait_ge(step, s.now())
        vec.tensor_scalar(self.mean[:, 1:2], self.mean[:, 1:2], EPS, None, ALU.add).then_inc(self.variance, 1)
        vec.wait_ge(self.deviation, j + 1)
        vec.reciprocal(self.inv[:, :], self.dev[:, :]).then_inc(step, s.one())
        vec.wait_ge(step, s.now())
        vec.tensor_scalar(m["x"][:, at(j), :].rearrange("p o f -> p (o f)"), self.new[:, :], self.mean[:, 0:1],
                          self.inv[:, :], ALU.subtract, ALU.mult).then_inc(step, s.one())
        vec.wait_ge(step, s.now())

    def tile(self, vec, j, slot):
        m, step, small = self.m, self.step, self.small
        s = Count(self.STEPS[self.kind] * j)
        sums = self.sums[slot]
        heads = sums[:, 0:FX].rearrange("p (h e) -> p h e", e=HX)
        new = self.new[:, :].rearrange("p (h d) -> p h d", d=HD)
        out = self.out[:, :].rearrange("p (h d) -> p h d", d=HD)
        x = m["x"][:, at(j), :].rearrange("p o f -> p (o f)")
        if self.kind == 0:
            vec.tensor_tensor(out, heads[:, :, 0:HD], m["bias0"][:, :].rearrange("p (h d) -> p h d", d=HD), ALU.add
                              ).then_inc(step, s.one())
            vec.wait_ge(step, s.now())
            vec.sem_inc(self.sums_used, 1)
            vec.scalar_tensor_tensor(self.new[:, :], self.out[:, :], 0.0, x, ALU.max, ALU.add
                                     ).then_inc(step, s.one())
            vec.wait_ge(step, s.now())
            self.normalize(vec, s, j)
        if self.kind == 1:
            vec.tensor_scalar(small[:, 0:4], heads[:, :, HD], 1e-30, None, ALU.max).then_inc(step, s.one())
            vec.wait_ge(step, s.now())
            vec.reciprocal(small[:, 4:8], small[:, 0:4]).then_inc(step, s.one())
            vec.wait_ge(step, s.now())
            vec.tensor_tensor(out, heads[:, :, 0:HD],
                              small[:, 4:8].rearrange("p (h o) -> p h o", o=1).to_broadcast([P, HEADS, HD]), ALU.mult
                              ).then_inc(step, s.one())
            vec.wait_ge(step, s.now())
            vec.sem_inc(self.sums_used, 1)
            vec.tensor_tensor(self.new[:, :], self.out[:, :], x, ALU.add).then_inc(step, s.one())
            vec.wait_ge(step, s.now())
            self.normalize(vec, s, j)
        if self.kind == 2:
            vec.tensor_scalar(small[:, 0:1], heads[:, 0, HD:HX], 1.0, None, ALU.max).then_inc(step, s.one())
            vec.wait_ge(step, s.now())
            vec.reciprocal(small[:, 1:2], small[:, 0:1]).then_inc(step, s.one())
            vec.wait_ge(step, s.now())
            vec.tensor_scalar(m["hx"][:, at(j), :].rearrange("p o (h e) -> p (o h) e", e=HX)[:, :, 0:HD],
                              heads[:, :, 0:HD], small[:, 1:2], None, ALU.mult).then_inc(self.sums_used, 1)
        if self.kind == 3:
            degree = heads[:, 0, HD:HX]
            vec.tensor_scalar(small[:, 0:1], degree, 0.0, None, ALU.is_gt).then_inc(step, s.one())
            vec.tensor_scalar(small[:, 1:2], degree, 0.0, None, ALU.is_le).then_inc(step, s.one())
            vec.wait_ge(step, s.now())
            vec.scalar_tensor_tensor(small[:, 2:3], degree, small[:, 0:1], small[:, 1:2], ALU.mult, ALU.add
                                     ).then_inc(step, s.one())
            vec.wait_ge(step, s.now())
            vec.reciprocal(small[:, 3:4], small[:, 2:3]).then_inc(step, s.one())
            vec.wait_ge(step, s.now())
            vec.tensor_tensor(small[:, 4:5], small[:, 3:4], small[:, 0:1], ALU.mult).then_inc(step, s.one())
            vec.wait_ge(step, s.now())
            vec.tensor_scalar(out, heads[:, :, 0:HD], small[:, 4:5], None, ALU.mult).then_inc(step, s.one())
            vec.wait_ge(step, s.now())
            vec.sem_inc(self.sums_used, 1)
            vec.tensor_tensor(self.new[:, :], self.out[:, :], x, ALU.add).then_inc(step, s.one())
            vec.wait_ge(step, s.now())
            vec.tensor_tensor(self.new[:, :], self.new[:, :], m["bias2"][:, :], ALU.add).then_inc(step, s.one())
            vec.wait_ge(step, s.now())
            self.normalize(vec, s, j)
        assert s.k == self.STEPS[self.kind]


def fast(eng, m, n):
    return eng.If(eng.value_load(m["flags"][0:1, n:n + 1], min_val=0, max_val=1) == 1)


class General:

    def __init__(self, nc, ctx, m, d, kind, sums, fin, bank=None):
        self.nc, self.m, self.d, self.kind, self.sums, self.fin, self.bank = nc, m, d, kind, sums[0], fin, bank
        taken = [0]

        def take(n):
            taken[0] += n
            return m["arena"][0:P, taken[0] - n:taken[0]]

        def sem(name):
            return ctx.enter_context(nc.semaphore(f"{name}_g{kind}"))

        self.loaded = sem("loaded")
        self.columns = sem("columns")
        self.ready = sem("ready")
        self.row_in = [sem(f"row_in{i}") for i in range(len(THIRDS))]
        self.message = sem("message")
        self.added = sem("added")
        self.step = sem("step")
        if kind == 1:
            self.edge_in = sem("edge_in")
            self.edge_read = sem("edge_read")
            self.apart = sem("apart")
            self.turned = sem("turned")
            self.best_in = sem("best_in")
            self.best_out = sem("best_out")
            self.top_in = sem("top_in")
            self.above = sem("above")
            self.weights = sem("weights")
        self.gather_index, self.sum_index, self.weight = take(GEN).bitcast(I32), take(GEN).bitcast(I32), take(GEN)
        self.local = take(GEN)
        self.coef = take(GEN * HEADS).rearrange("p (c h) -> p c h", h=HEADS)
        self.now = [take(1).bitcast(I32) for _ in range(2)]
        self.ends = [take(HEADS) for _ in range(2)]
        self.row, self.scaled, self.zero = take(FX), take(FX), take(FX)
        self.onehot, self.low = take(P), take(P)
        self.logits = take(P * HEADS).rearrange("p (h n) -> p h n", n=P)
        self.found = take(HEADS)
        self.best = take(TILES * HEADS).rearrange("p (t h) -> p t h", h=HEADS)

    def gpsimd(self, pool):
        m, d, nc = self.m, self.d, self.nc
        gather, add = ("src", "dst") if self.kind == 2 else ("dst", "src")
        pool.memset(self.zero, 0.0).then_inc(self.columns, 1)
        if self.kind == 0:
            pool.memset(m["hx"][:, :, :].rearrange("p t (h e) -> p t h e", e=HX)[:, :, :, HD], 1.0
                        ).then_inc(self.columns, 1)
            pool.wait_ge(self.columns, 2)
        pool.dma_start(self.gather_index, d[gather].rearrange("(p c) -> p c", c=GEN)).then_inc(self.loaded, 16)
        pool.dma_start(self.sum_index, d[add].rearrange("(p c) -> p c", c=GEN)).then_inc(self.loaded, 16)
        pool.dma_start(self.weight, d["ew"].rearrange("(p c) -> p c", c=GEN)).then_inc(self.loaded, 16)
        pool.dma_start(d["targets"].rearrange("(t p) e -> p t e", p=P), m["hx"][:, :, :]).then_inc(self.loaded, 16)
        if self.kind == 1:
            with nc.allow_non_contiguous_dma(reason="50 KB each, once"):
                for name, half in (("sources", "hl"), ("halves", "hr")):
                    pool.dma_start(d[name].rearrange("(t p) h -> p t h", p=P), m[half][:, :, :]
                                   ).then_inc(self.loaded, 16)
        pool.wait_ge(self.loaded, 96 if self.kind == 1 else 64)

        def index(k, column, c):
            return pool.tensor_copy(self.now[k], column[:, bass.ds(c, 1)])

        def rows(out, table, k):
            return pool.indirect_dma_start(out, None, d[table], bass.IndirectOffsetOnAxis(self.now[k], 0))

        if self.kind == 1:
            with pool.Fori(0, GEN) as c:
                pool.wait_ge(self.edge_read, CREDIT + c)
                index(0, self.sum_index, c)
                index(1, self.gather_index, c)
                pool.drain()
                rows(self.ends[0], "sources", 0).then_inc(self.edge_in, 16)
                rows(self.ends[1], "halves", 1).then_inc(self.edge_in, 16)
            pool.wait_ge(self.best_in, 1)
            with nc.allow_non_contiguous_dma(reason="50 KB, once"):
                pool.dma_start(d["tops"].rearrange("(t p) h -> p t h", p=P), self.best).then_inc(self.best_out, 16)
            pool.wait_ge(self.best_out, 16)
            with pool.Fori(0, GEN) as c:
                pool.wait_ge(self.weights, CREDIT + c)
                index(0, self.sum_index, c)
                pool.drain()
                rows(self.ends[0], "tops", 0).then_inc(self.top_in, 16)
        for third, (first, count) in enumerate(THIRDS):
            with pool.Fori(0, count) as t:
                with pool.Fori(0, GEN) as c:
                    pool.wait_ge(self.message, CREDIT + GEN * (t + first) + c)
                    index(1, self.gather_index, c)
                    pool.drain()
                    rows(self.row, "targets", 1).then_inc(self.row_in[third], 16)

    def vector(self, vec):
        m, kind, step = self.m, self.kind, self.step
        n = Count()
        vec.sem_inc(self.message, CREDIT)
        vec.sem_inc(self.added, CREDIT)
        if kind == 1:
            vec.sem_inc(self.edge_read, CREDIT)
            vec.sem_inc(self.weights, CREDIT)
            vec.sem_inc(self.turned, CREDIT)
        vec.wait_ge(self.loaded, 96 if kind == 1 else 64)
        vec.tensor_copy(self.local, self.sum_index).then_inc(self.ready, n.one())
        if kind == 0:
            vec.tensor_copy(self.coef, self.weight.rearrange("p (c o) -> p c o", o=1).to_broadcast([P, GEN, HEADS])
                            ).then_inc(self.ready, n.one())
        else:
            vec.memset(self.coef, 1.0).then_inc(self.ready, n.one())
        vec.memset(self.best, -3e38).then_inc(self.ready, n.one())
        vec.wait_ge(self.ready, n.now())

        def node_hot(c):
            return vec.tensor_scalar(self.onehot, m["one_up"][0:P, 0:P], self.local[:, bass.ds(c, 1)], None,
                                     ALU.is_equal)

        vec.tensor_scalar(self.local, self.local, 1.0 + P, None, ALU.add).then_inc(self.ready, n.one())
        vec.wait_ge(self.ready, n.now())
        if kind == 1:
            a, b = self.ends
            with vec.Fori(0, GEN) as c:
                s = Count(2 * c)
                z = self.coef[:, bass.ds(c, 1), :].rearrange("p o h -> p (o h)")
                vec.wait_ge(self.edge_in, 32 * c + 32)
                vec.tensor_tensor(z, a, b, ALU.add).then_inc(step, s.one())
                vec.wait_ge(step, s.now())
                vec.scalar_tensor_tensor(z, z, 0.2, z, ALU.mult, ALU.max).then_inc(step, s.one())
                vec.wait_ge(step, s.now())
                vec.sem_inc(self.edge_read, 1)
            with vec.Fori(0, TILES) as t:
                vec.tensor_scalar(self.local, self.local, -float(P), None, ALU.add)
                vec.drain()
                with vec.Fori(0, GEN) as c:
                    k = GEN * t + c
                    s = Count(2 * GEN + 8 * k)
                    best = self.best[:, at(t), :].rearrange("p o h -> p (o h)")
                    node_hot(c).then_inc(step, s.one())
                    vec.wait_ge(step, s.now())
                    vec.tensor_scalar(self.low, self.onehot, -1.0, 3e38, ALU.add, ALU.mult).then_inc(step, s.one())
                    vec.wait_ge(step, s.now())
                    for h in range(HEADS):
                        vec.tensor_scalar(self.logits[:, h, :], self.low, self.coef[:, bass.ds(c, 1), h], None,
                                          ALU.add).then_inc(step, s.one())
                    vec.wait_ge(step, s.now())
                    vec.sem_inc(self.apart, 1)
                    vec.wait_ge(self.turned, CREDIT + k + 1)
                    vec.tensor_reduce(self.found, self.bank[0:P, 0:HEADS * P].rearrange("p (h n) -> p h n", n=P), AX.X,
                                      ALU.max).then_inc(step, s.one())
                    vec.wait_ge(step, s.now())
                    vec.tensor_tensor(best, best, self.found, ALU.max).then_inc(step, s.one())
                    vec.wait_ge(step, s.now())
            vec.sem_inc(self.best_in, 1)
            with vec.Fori(0, GEN) as c:
                z = self.coef[:, bass.ds(c, 1), :].rearrange("p o h -> p (o h)")
                vec.wait_ge(self.top_in, 16 * c + 16)
                vec.tensor_tensor(z, z, a, ALU.subtract).then_inc(self.above, 1)
                vec.wait_ge(self.weights, CREDIT + c + 1)
            vec.tensor_scalar(self.local, self.local, float(P * TILES), None, ALU.add)
            vec.drain()
        chunks_before = (2 + 8 * TILES) * GEN if kind == 1 else 0
        for third, (first, count) in enumerate(THIRDS):
            with vec.Fori(0, count) as t:
                vec.tensor_scalar(self.local, self.local, -float(P), None, ALU.add)
                vec.drain()
                with vec.Fori(0, GEN) as c:
                    k = GEN * (t + first) + c
                    s = Count(chunks_before + 2 * k)
                    vec.wait_ge(self.row_in[third], 16 * (GEN * t + c) + 16)
                    vec.wait_ge(self.added, CREDIT + k)
                    node_hot(c).then_inc(step, s.one())
                    vec.tensor_tensor(
                        self.scaled.rearrange("p (h e) -> p h e", e=HX), self.row.rearrange("p (h e) -> p h e", e=HX),
                        self.coef[:, bass.ds(c, 1), :].rearrange("p o (h e) -> p (o h) e", e=1).to_broadcast(
                            [P, HEADS, HX]), ALU.mult).then_inc(step, s.one())
                    vec.wait_ge(step, s.now())
                    vec.sem_inc(self.message, 1)
                vec.wait_ge(self.added, CREDIT + GEN * (t + first) + GEN)
                self.fin.tile(vec, t + first, 0)

    def scalar(self, act):
        if self.kind == 1:
            with act.Fori(0, GEN) as c:
                z = self.coef[:, bass.ds(c, 1), :].rearrange("p o h -> p (o h)")
                act.wait_ge(self.above, c + 1)
                act.activation(z, z, ACT.Exp).then_inc(self.weights, 1)
        if self.kind != 2:
            with act.Fori(0, TILES) as t:
                self.fin.sqrt(act, t)

    def tensor(self, pe):
        if self.kind == 1:
            with pe.Fori(0, TILES * GEN) as k:
                pe.wait_ge(self.apart, k + 1)
                for h in range(HEADS):
                    last = pe.transpose(self.bank[0:P, h * P:(h + 1) * P], self.logits[:, h, :],
                                        self.m["ident"][0:P, 0:P])
                last.then_inc(self.turned, 1)
        pe.wait_ge(self.columns, 1)
        with pe.Fori(0, TILES) as t:
            pe.wait_ge(self.fin.sums_used, CREDIT + t)
            pe.matmul(self.sums[:, 0:FX], self.zero[:, 0:P], self.zero[:, 0:FX], start=True, stop=False,
                      skip_group_check=True)
            with pe.Fori(0, GEN) as c:
                pe.wait_ge(self.message, CREDIT + GEN * t + c + 1)
                pe.matmul(self.sums[:, 0:FX], self.onehot, self.scaled, start=False, stop=True,
                          skip_group_check=True).then_inc(self.added, 1)

    def sync(self, sync):
        sync.nop()


def sum_layer(nc, m, d, kind):
    with ExitStack() as ctx:
        def sem(name):
            return ctx.enter_context(nc.semaphore(f"{name}_{kind}"))

        hot = sem("hot")
        weighted = sem("weighted")
        block_done = sem("block_done")
        block_kept = sem("block_kept")
        summed = sem("summed")
        dt = F32 if kind == 0 else BF16
        words = TILES * P if kind == 0 else TILES * P // 2 + 1

        def area(n):
            part = m["arena"][:, n * words:(n + 1) * words]
            part = part if dt == F32 else part.bitcast(dt)
            return part[:, 0:TILES * P].rearrange("p (i n) -> p i n", n=P)

        by_source, by_target = area(0), area(1)
        kept = [ctx.enter_context(nc.sbuf_tensor(f"kept_{kind}_{i}", [P, 4, P], dt)) for i in range(2)]
        dense = [ctx.enter_context(nc.psum_tensor(f"dense_{kind}_{i}", [P, 512], F32)) for i in range(2)]
        sums = [ctx.enter_context(nc.psum_tensor(f"sums_{kind}_{i}", [P, 512], F32)) for i in range(2)]
        fin = Finish(nc, ctx, m, kind, sums)
        slow = General(nc, ctx, m, d, kind, sums, fin)
        rows, columns = (by_source, by_target) if kind == 2 else (by_target, by_source)
        block = ctx.enter_context(nc.Block())

        @block.vector
        def _(vec):
            def onehots(t, half):
                i, n = START[half], HALF[half]

                def of_bucket(k):
                    if kind == 2:
                        one = m["table"][:, k, i:i + n, at(t)]
                    else:
                        one = m["table"][:, k, at(t), i:i + n].rearrange("p o (n b) -> p (o n) b", b=1)
                    return one.to_broadcast([128, n, P])

                nodes = m["one_up"][:, 0:P].rearrange("p (o n) -> p o n", o=1).to_broadcast([128, n, P])
                vec.wait_ge(block_done, 8 * t + CREDIT - 4 + 4 * half)
                vec.tensor_tensor(by_target[:, i:i + n, :], of_bucket(1), nodes, ALU.is_equal).then_inc(hot, 1)
                if kind == 0:
                    vec.tensor_tensor(by_source[:, i:i + n, :], of_bucket(0), nodes, ALU.is_equal
                                      ).then_inc(weighted, 1)
                    vec.wait_ge(weighted, 2 * t + half + 1)
                    vec.tensor_tensor(by_source[:, i:i + n, :], by_source[:, i:i + n, :], of_bucket(2), ALU.mult
                                      ).then_inc(hot, 1)
                else:
                    vec.tensor_tensor(by_source[:, i:i + n, :], of_bucket(0), nodes, ALU.is_equal).then_inc(hot, 1)

            def tile(t, slot, more):
                if more:
                    onehots(t + 1, 0)
                    onehots(t + 1, 1)
                vec.wait_ge(summed, CREDIT + 8 * t + 8)
                fin.tile(vec, t, slot)

            vec.sem_inc(block_done, CREDIT)
            vec.sem_inc(fin.sums_used, CREDIT)
            with fast(vec, m, 0):
                onehots(0, 0)
                onehots(0, 1)
                in_pairs(vec, tile)
            with vec.Else():
                slow.vector(vec)
            vec.nop()

        @block.tensor
        def _(pe):
            def blocks(t, g):
                q, (i, n) = 8 * t + g, GROUPS[g]
                if g in (0, 4):
                    pe.wait_ge(hot, 4 * t + (2 if g == 0 else 4))
                pe.wait_ge(block_kept, CREDIT + q - 1)
                for b in range(n):
                    last = pe.matmul(dense[g % 2][:, b * P:(b + 1) * P], rows[:, i + b, :], columns[:, i + b, :],
                                     start=True, stop=True)
                last.then_inc(block_done, 1)

            def products(t, slot, g):
                q, (i, n) = 8 * t + g, GROUPS[g]
                pe.wait_ge(block_kept, CREDIT + q + 1)
                if g == 0:
                    pe.wait_ge(fin.sums_used, CREDIT + t - 1)
                for b in range(n):
                    if kind == 0:
                        heads = "p (h e) -> p h e"
                        last = pe.matmul(sums[slot][:, 0:FX].rearrange(heads, e=HX)[:, :, 0:HD], kept[g % 2][:, b, :],
                                         m["hx"][:, i + b, :].rearrange(heads, e=HX)[:, :, 0:HD],
                                         start=i + b == 0, stop=i + b == TILES - 1)
                    else:
                        for part in range(3):
                            last = pe.matmul(sums[slot][:, 0:FX], kept[g % 2][:, b, :], m["hs"][:, part, i + b, :],
                                             start=i + b == 0 and part == 0, stop=i + b == TILES - 1 and part == 2)
                last.then_inc(summed, 1)

            def tile(t, slot, more):
                for g in range(8):
                    if g < 7:
                        blocks(t, g + 1)
                    elif more:
                        blocks(t + 1, 0)
                    products(t, slot, g)

            pe.sem_inc(summed, CREDIT)
            with fast(pe, m, 0):
                blocks(0, 0)
                in_pairs(pe, tile)
            with pe.Else():
                slow.tensor(pe)
            pe.nop()

        @block.scalar
        def _(act):
            def keep(t, g):
                q, n = 8 * t + g, GROUPS[g][1]
                act.wait_ge(block_done, CREDIT + q + 1)
                act.wait_ge(summed, CREDIT + q - 1)
                act.copy(kept[g % 2][:, 0:n, :], dense[g % 2][:, 0:n * P].rearrange("p (b n) -> p b n", n=P)
                         ).then_inc(block_kept, 1)

            def tile(t, slot, more):
                for g in range(3, 8):
                    keep(t, g)
                if more:
                    for g in range(3):
                        keep(t + 1, g)
                if kind != 2:
                    fin.sqrt(act, t)

            act.sem_inc(block_kept, CREDIT)
            with fast(act, m, 0):
                for g in range(3):
                    keep(0, g)
                in_pairs(act, tile)
            with act.Else():
                slow.scalar(act)
            act.nop()

        @block.gpsimd
        def _(pool):
            with fast(pool, m, 0):
                pool.nop()
            with pool.Else():
                slow.gpsimd(pool)
            pool.nop()


def attention_layer(nc, m, d):
    with ExitStack() as ctx:
        def sem(name):
            return ctx.enter_context(nc.semaphore(f"{name}_1"))

        def sb(name, shape, dt=F32):
            return ctx.enter_context(nc.sbuf_tensor(f"{name}_1", shape, dt))

        rows_in = [sem(f"rows_in{h}") for h in range(2)]
        gathers_hot = sem("gathers_hot")
        sums_hot = sem("sums_hot")
        logits_done = sem("logits_done")
        logits_read = sem("logits_read")
        step = sem("step")
        exponent = sem("exponent")
        weights = sem("weights")
        gathered = sem("gathered")
        scaled = sem("scaled")
        summed = sem("summed")
        room = 13 * 128 // 2
        arena = m["arena"]

        def part(n):
            return arena[0:P, n * room:(n + 1) * room].bitcast(BF16)

        rows = {(k, h): part(2 * k + h) for k in range(2) for h in range(2)}
        to_edges = {(k, h): part(4 + 2 * k + h) for k in range(2) for h in range(2)}
        to_nodes = arena[:, 8 * room:8 * room + TILES * P].rearrange("p (i n) -> p i n", n=P)
        mine = [sb(f"mine{h}", [128, 13]) for h in range(2)]
        logits = [sb(f"logits{h}", [128, 13, 12]) for h in range(2)]
        expo = [sb(f"expo{h}", [128, 13, HEADS]) for h in range(2)]
        scale = [sb(f"scale{h}", [128, 13, HEADS]) for h in range(2)]
        message = [sb(f"message{i}", [128, FX]) for i in range(5)]
        sums = [ctx.enter_context(nc.psum_tensor(f"sums_1_{i}", [P, 512], F32)) for i in range(2)]
        edge_rows = [ctx.enter_context(nc.psum_tensor(f"edge_rows{i}", [128, 512], F32)) for i in range(5)]
        edge_logits = ctx.enter_context(nc.psum_tensor("edge_logits", [128, 512], F32))
        parts = edge_logits[:, 0:13 * 36].rearrange("p (i s c) -> p i s c", s=3, c=12)
        fin = Finish(nc, ctx, m, 1, sums)
        slow = General(nc, ctx, m, d, 1, sums, fin, edge_logits)
        block = ctx.enter_context(nc.Block())

        def following(t, half):
            return (t, 1) if half == 0 else (t + 1, 0)

        @block.sync
        def _(sync):
            def load(t, half):
                i, n = START[half], HALF[half]
                sync.wait_ge(gathers_hot, CREDIT + 4 * t + 2 * half - 2)
                for k in range(2):
                    sync.dma_start(rows[k, half][:, 0:n * RANKS],
                                   d["rows"][k, bass.ds(TILES * t + i, n), :].rearrange("i r -> (i r)")
                                   .partition_broadcast(P)).then_inc(rows_in[half], 16)

            def tile(t, slot, more):
                load(t, 0)
                load(t, 1)

            with fast(sync, m, 1):
                in_pairs(sync, tile)
            with sync.Else():
                slow.sync(sync)
            sync.nop()

        @block.gpsimd
        def _(pool):
            def onehots(t, half):
                i, n = START[half], HALF[half]
                pool.wait_ge(sums_hot, CREDIT + 2 * t + half - 1)
                pool.wait_ge(summed, TILES * t + (32 - TILES + i + n))
                pool.tensor_copy(mine[half][:, 0:n], m["table"][:, 0, at(t), i:i + n].rearrange("p o n -> p (o n)")
                                 )
                pool.drain()
                for b in range(n):
                    last = pool.tensor_scalar(to_nodes[:, i + b, :], m["one_up"][:, 0:P], mine[half][:, b:b + 1],
                                              None, ALU.is_equal)
                last.then_inc(sums_hot, 1)

            def tile(t, slot, more):
                onehots(t, 0)
                onehots(t, 1)

            pool.sem_inc(sums_hot, CREDIT)
            with fast(pool, m, 1):
                in_pairs(pool, tile)
            with pool.Else():
                slow.gpsimd(pool)
            pool.nop()

        @block.vector
        def _(vec):
            def onehots(t, half):
                n = HALF[half]
                vec.wait_ge(rows_in[half], 32 * t + 32)
                vec.wait_ge(gathered, TILES * t + (32 - TILES + START[half] + n))
                for k in range(2):
                    vec.tensor_scalar(to_edges[k, half][:, 0:n * RANKS], rows[k, half][:, 0:n * RANKS],
                                      m["row"][0:P, :], None, ALU.is_equal).then_inc(gathers_hot, 1)

            def exponents(t, half):
                n, u = HALF[half], 2 * t + half
                s = Count(3 * u)
                all_parts, e = logits[half][:, 0:n, :], expo[half][:, 0:n, :]
                vec.wait_ge(logits_done, u + 1)
                vec.tensor_reduce(all_parts, parts[:, 0:n, :, :].rearrange("p i s c -> p i c s"), AX.X, ALU.add
                                  ).then_inc(logits_read, 1)
                vec.wait_ge(logits_read, CREDIT + u + 1)
                vec.wait_ge(weights, CREDIT + u - 1)
                vec.tensor_tensor(e, all_parts[:, :, 0:4], all_parts[:, :, 8:12], ALU.add).then_inc(step, s.one())
                vec.wait_ge(step, s.now())
                vec.scalar_tensor_tensor(e, e, 0.2, e, ALU.mult, ALU.max).then_inc(step, s.one())
                vec.wait_ge(step, s.now())
                vec.tensor_tensor(e, e, all_parts[:, :, 4:8], ALU.subtract).then_inc(exponent, 1)
                vec.sem_inc(step, s.one())

            def messages(t, half, start, stop):
                vec.wait_ge(weights, CREDIT + 2 * t + half + 1)
                for b in range(start, stop):
                    i = START[half] + b
                    vec.wait_ge(gathered, 32 + TILES * t + i + 1)
                    vec.wait_ge(summed, 32 + TILES * t + i - 4)
                    vec.tensor_tensor(
                        message[i % 5][:, :].rearrange("p (h e) -> p h e", e=HX),
                        edge_rows[i % 5][:, 0:FX].rearrange("p (h e) -> p h e", e=HX),
                        scale[half][:, b, :].rearrange("p (h o) -> p h o", o=1).to_broadcast([128, HEADS, HX]),
                        ALU.mult).then_inc(scaled, 1)

            def unit(t, half, slot, more):
                nxt = following(t, half) if more or half == 0 else None
                messages(t, half, 0, 3)
                if nxt:
                    onehots(*nxt)
                messages(t, half, 3, 9)
                if nxt:
                    exponents(*nxt)
                messages(t, half, 9, HALF[half])

            def tile(t, slot, more):
                unit(t, 0, slot, more)
                unit(t, 1, slot, more)
                vec.wait_ge(summed, 32 + TILES * (t + 1))
                fin.tile(vec, t, slot)

            vec.sem_inc(gathers_hot, CREDIT)
            vec.sem_inc(logits_read, CREDIT)
            vec.sem_inc(fin.sums_used, CREDIT)
            with fast(vec, m, 1):
                onehots(0, 0)
                exponents(0, 0)
                in_pairs(vec, tile)
            with vec.Else():
                slow.vector(vec)
            vec.nop()

        @block.scalar
        def _(act):
            def tile(t, slot, more):
                for half in range(2):
                    if half == 0 or more:
                        nt, nh = following(t, half)
                        act.wait_ge(exponent, 2 * nt + nh + 1)
                        act.activation(scale[nh][:, 0:HALF[nh], :], expo[nh][:, 0:HALF[nh], :], ACT.Exp
                                       ).then_inc(weights, 1)
                fin.sqrt(act, t)

            act.sem_inc(weights, CREDIT)
            with fast(act, m, 1):
                act.wait_ge(exponent, 1)
                act.activation(scale[0][:, 0:HALF[0], :], expo[0][:, 0:HALF[0], :], ACT.Exp).then_inc(weights, 1)
                in_pairs(act, tile)
            with act.Else():
                slow.scalar(act)
            act.nop()

        @block.tensor
        def _(pe):
            def gather_logits(t, half):
                i, n = START[half], HALF[half]
                pe.wait_ge(gathers_hot, CREDIT + 4 * t + 2 * half + 2)
                pe.wait_ge(logits_read, CREDIT + 2 * t + half)
                for b in range(n):
                    edges = slice(b * RANKS, (b + 1) * RANKS)
                    pe.matmul(parts[:, b, :, 0:8], to_edges[0, half][:, edges],
                              m["logit"][:, at(t), :, 0:8].rearrange("p o s c -> p (o s) c"), start=True, stop=True)
                    last = pe.matmul(parts[:, b, :, 8:12], to_edges[1, half][:, edges],
                                     m["logit"][:, i + b, :, 8:12], start=True, stop=True)
                last.then_inc(logits_done, 1)

            def gather(t, half, b):
                i = START[half] + b
                pe.wait_ge(scaled, 32 + TILES * t + i - 4)
                for part in range(3):
                    last = pe.matmul(edge_rows[i % 5][:, 0:FX], to_edges[1, half][:, b * RANKS:(b + 1) * RANKS],
                                     m["hs"][:, part, i, :], start=part == 0, stop=part == 2)
                last.then_inc(gathered, 1)

            def add(t, half, slot, b):
                i = START[half] + b
                if b == 0:
                    pe.wait_ge(sums_hot, CREDIT + 2 * t + half + 1)
                if i == 0:
                    pe.wait_ge(fin.sums_used, CREDIT + t - 1)
                pe.wait_ge(scaled, 32 + TILES * t + i + 1)
                pe.matmul(sums[slot][:, 0:FX], to_nodes[:, i, :], message[i % 5][:, :],
                          start=i == 0, stop=i == TILES - 1).then_inc(summed, 1)

            def unit(t, half, slot, more):
                n = HALF[half]
                for b in range(n + 3):
                    if b < n:
                        gather(t, half, b)
                    if b >= 3:
                        add(t, half, slot, b - 3)
                    if b == 8 and (more or half == 0):
                        gather_logits(*following(t, half))

            def tile(t, slot, more):
                unit(t, 0, slot, more)
                unit(t, 1, slot, more)

            pe.sem_inc(scaled, 32)
            pe.sem_inc(summed, 32)
            pe.sem_inc(gathered, 32)
            with fast(pe, m, 1):
                gather_logits(0, 0)
                in_pairs(pe, tile)
            with pe.Else():
                slow.tensor(pe)
            pe.nop()


def last_layer(nc, m, d):
    with ExitStack() as ctx:
        def sem(name):
            return ctx.enter_context(nc.semaphore(f"{name}_l"))

        def sb(name, shape, dt=F32, n=2):
            return [ctx.enter_context(nc.sbuf_tensor(f"{name}_l{i}", shape, dt)) for i in range(n)]

        ends_in = sem("ends_in")
        placed = sem("placed")
        stored = sem("stored")
        rows_in = [sem(f"rows_in{i}") for i in range(2)]
        step = sem("step")
        top = sem("top")
        raised = sem("raised")
        variance = sem("variance")
        deviation = sem("deviation")
        ready = sem("ready")
        written = [sem(f"written{i}") for i in range(2)]
        ends = [ctx.enter_context(nc.sbuf_tensor(f"ends_l{i}", [P, TILES], I32)) for i in range(2)]
        target, source = sb("target", [P, FX]), sb("source", [P, HEADS])
        now = [sb(f"now{i}", [P, 1], I32) for i in range(2)]
        logit, power = sb("logit", [P, HEADS]), sb("power", [P, HEADS])
        small = sb("small", [P, 4])
        mean, stats = sb("mean", [P, 2]), sb("stats", [P, 6])
        dev = sb("dev", [P, 1])
        scaled, one_head = sb("scaled", [P, F]), sb("one_head", [P, HD])
        new, out = sb("new", [P, F]), sb("out", [P, F])
        hxv = m["hx"][:, :, :].rearrange("p t (h e) -> p t h e", e=HX)
        block = ctx.enter_context(nc.Block())
        PER = 13

        @block.sync
        def _(sync):
            with nc.allow_non_contiguous_dma(reason="12.5 KB each, once"):
                sync.dma_start(ends[0][:, :], d["src"][0:N].rearrange("(t p) -> p t", p=P)).then_inc(ends_in, 16)
                sync.dma_start(ends[1][:, :], d["dst"][0:N].rearrange("(t p) -> p t", p=P)).then_inc(ends_in, 16)
            sync.wait_ge(placed, 1)
            sync.dma_start(d["targets"].rearrange("(t p) e -> p t e", p=P), m["hx"][:, :, :]).then_inc(stored, 16)
            with nc.allow_non_contiguous_dma(reason="50 KB, once"):
                sync.dma_start(d["sources"].rearrange("(t p) h -> p t h", p=P), m["hl"][:, :, :]).then_inc(stored, 16)

            def write(t, slot, more):
                sync.wait_ge(ready, t + 1)
                sync.dma_start(d["out"][bass.ds(P * t, P), :], out[slot][:, :]).then_inc(written[slot], 16)

            in_pairs(sync, write)
            sync.wait_ge(written[0], CREDIT + 16 * 13)
            sync.wait_ge(written[1], CREDIT + 16 * 12)

        @block.gpsimd
        def _(pool):
            pool.tensor_copy(hxv[:, :, :, HD], m["hr"][:, :, :]).then_inc(placed, 1)
            pool.wait_ge(ends_in, 32)
            pool.wait_ge(stored, 32)

            def gather(t, slot, more):
                pool.wait_ge(step, PER * t + 16 - PER)
                for k in range(2):
                    pool.tensor_copy(now[k][slot][:, :], ends[k][:, at(t)])
                pool.drain()
                pool.indirect_dma_start(source[slot][:, :], None, d["sources"],
                                        bass.IndirectOffsetOnAxis(now[0][slot][:, 0:1], 0)).then_inc(rows_in[slot], 16)
                pool.indirect_dma_start(target[slot][:, :], None, d["targets"],
                                        bass.IndirectOffsetOnAxis(now[1][slot][:, 0:1], 0)).then_inc(rows_in[slot], 16)

            in_pairs(pool, gather)

        @block.scalar
        def _(act):
            def tile(t, slot, more):
                act.wait_ge(top, t + 1)
                act.activation(power[slot][:, :], logit[slot][:, :], ACT.Exp).then_inc(raised, 1)
                act.wait_ge(variance, t + 1)
                act.activation(dev[slot][:, :], mean[slot][:, 1:2], ACT.Sqrt).then_inc(deviation, 1)

            in_pairs(act, tile)

        @block.vector
        def _(vec):
            def tile(t, slot, more):
                s = Count(16 + PER * t)
                row = target[slot][:, :].rearrange("p (h e) -> p h e", e=HX)
                z, w = logit[slot][:, :], power[slot][:, :]
                k = small[slot]
                scaled_heads = scaled[slot][:, :].rearrange("p (h d) -> p h d", d=HD)
                vec.wait_ge(rows_in[slot], 16 * t + 32 - 16 * slot)
                vec.tensor_tensor(z, source[slot][:, :], row[:, :, HD], ALU.add).then_inc(step, s.one())
                vec.wait_ge(step, s.now())
                vec.scalar_tensor_tensor(z, z, 0.01, z, ALU.mult, ALU.max).then_inc(step, s.one())
                vec.wait_ge(step, s.now())
                vec.tensor_reduce(k[:, 0:1], z, AX.X, ALU.max).then_inc(step, s.one())
                vec.wait_ge(step, s.now())
                vec.tensor_scalar(z, z, k[:, 0:1], None, ALU.subtract).then_inc(top, 1)
                vec.wait_ge(raised, t + 1)
                vec.tensor_reduce(k[:, 1:2], w, AX.X, ALU.add).then_inc(step, s.one())
                vec.wait_ge(step, s.now())
                vec.reciprocal(k[:, 2:3], k[:, 1:2]).then_inc(step, s.one())
                vec.wait_ge(step, s.now())
                vec.tensor_scalar(w, w, k[:, 2:3], None, ALU.mult).then_inc(step, s.one())
                vec.wait_ge(step, s.now())
                vec.tensor_tensor(scaled_heads, row[:, :, 0:HD],
                                  w.rearrange("p (h o) -> p h o", o=1).to_broadcast([P, HEADS, HD]), ALU.mult
                                  ).then_inc(step, s.one())
                vec.wait_ge(step, s.now())
                vec.tensor_reduce(one_head[slot][:, :], scaled_heads.rearrange("p h d -> p d h"), AX.X, ALU.add
                                  ).then_inc(step, s.one())
                vec.wait_ge(step, s.now())
                vec.tensor_tensor(new[slot][:, :].rearrange("p (h d) -> p h d", d=HD),
                                  m["x"][:, at(t), :].rearrange("p o (h d) -> p (o h) d", d=HD),
                                  one_head[slot][:, :].rearrange("p (o d) -> p o d", o=1).to_broadcast([P, HEADS, HD]),
                                  ALU.add).then_inc(step, s.one())
                vec.wait_ge(step, s.now())
                vec.bn_stats(stats[slot][:, :], new[slot][:, :]).then_inc(step, s.one())
                vec.drain()
                vec.bn_aggr(mean[slot][:, :], stats[slot][:, :]).then_inc(step, s.one())
                vec.wait_ge(step, s.now())
                vec.tensor_scalar(mean[slot][:, 1:2], mean[slot][:, 1:2], EPS, None, ALU.add).then_inc(variance, 1)
                vec.wait_ge(deviation, t + 1)
                vec.reciprocal(k[:, 3:4], dev[slot][:, :]).then_inc(step, s.one())
                vec.wait_ge(step, s.now())
                vec.wait_ge(written[slot], 8 * t + CREDIT - 8 * slot)
                vec.tensor_scalar(out[slot][:, :], new[slot][:, :], mean[slot][:, 0:1], k[:, 3:4], ALU.subtract,
                                  ALU.mult).then_inc(ready, 1)
                vec.sem_inc(step, s.one())
                assert s.k == 13

            vec.sem_inc(written[0], CREDIT)
            vec.sem_inc(written[1], CREDIT)
            vec.sem_inc(step, 16)
            in_pairs(vec, tile)


def program(nc, d):
    with ExitStack() as ctx:
        m = tensors(nc, ctx)
        load_and_starts(nc, m, d)
        build_table(nc, m, d)
        project(nc, m, 0, 0, split=False)
        sum_layer(nc, m, d, 0)
        project(nc, m, 1, 1, split=True, attn=0)
        attention_inputs(nc, m)
        attention_layer(nc, m, d)
        project(nc, m, 2, 2, split=True)
        sum_layer(nc, m, d, 2)
        split_edges(nc, m)
        sum_layer(nc, m, d, 3)
        project(nc, m, 3, 3, split=False, attn=2)
        last_layer(nc, m, d)


_INS = {"x": "x", "src": "src", "dst": "dst", "ew": "edge_weight", "nv": "node_vec", "w0": "L0_gnn_kernel",
        "bias0": "L0_gnn_bias", "w1": "L1_gnn_W", "al1": "L1_gnn_a_l", "ar1": "L1_gnn_a_r", "w2": "L2_gnn_W",
        "bias2": "L2_gnn_b", "w3": "L3_gnn_weight", "al3": "L3_gnn_attn_l", "ar3": "L3_gnn_attn_r"}
_SCRATCH = {"rows": ((2, TILES * TILES, RANKS), BF16), "targets": ((N, FX), F32),
            "sources": ((N, HEADS), F32), "halves": ((N, HEADS), F32),
            "tops": ((N, HEADS), F32)}


def kernel(**inputs):
    import numpy as _np
    import concourse.bacc as _bacc
    from concourse import mybir as _mybir
    from concourse.bass_utils import run_bass_kernel_spmd as _run

    nc = _bacc.Bacc("TRN2", target_bir_lowering=False, num_devices=1)
    arrays, d = {}, {}
    for short, name in _INS.items():
        a = _np.ascontiguousarray(inputs[name])
        if short[:2] in ("al", "ar"):
            a = a.reshape(-1)
        arrays[f"in_{short}"] = a
        d[short] = nc.dram_tensor(f"in_{short}", a.shape, _mybir.dt.from_np(a.dtype), kind="ExternalInput").ap()
    for name, (shape, dtype) in _SCRATCH.items():
        d[name] = nc.dram_tensor(f"{name}_dram", shape, dtype).ap()
    d["out"] = nc.dram_tensor("out_dram", (N, F), F32, kind="ExternalOutput").ap()
    program(nc, d)
    r = _run(nc, [arrays], core_ids=[0])
    return r.results[0]["out_dram"]
```

```python
from contextlib import ExitStack

import numpy as np

import concourse.bass as bass
from concourse import mybir

F32 = mybir.dt.float32
BF16 = mybir.dt.bfloat16
F32R = mybir.dt.float32r
I32 = mybir.dt.int32
ALU = mybir.AluOpType
ACT = mybir.ActivationFunctionType
AX = mybir.AxisListType

N, E, F = 3125, 50000, 256
TILES, P = 25, 125
HEADS, HD = 4, 64
HX = HD + 1
FX = HEADS * HX
CH = 18
WIN = CH * 128
RANKS = 128
PAY = 5
GEN = E // P
HALF = [12, 13]
START = [0, 12]
GROUPS = [(0, 3), (3, 3), (6, 3), (9, 3), (12, 3), (15, 3), (18, 3), (21, 4)]
CREDIT = 8
LAG = 5
THIRDS = [(0, 9), (9, 9), (18, 7)]
ARENA = 5000
MAGIC = 12582912.0
EPS = 1e-5
SPREAD = 60.0


class Count:

    def __init__(self, base=0):
        self.base, self.k = base, 0

    def one(self):
        self.k += 1
        return 1

    def now(self):
        return self.base + self.k


def at(i):
    return bass.ds(i, 1)


def tensors(nc, ctx):
    def sb(name, shape, dt=F32):
        return ctx.enter_context(nc.sbuf_tensor(name, shape, dt))

    m = {}
    m["x"] = sb("x_sb", [P, TILES, F])
    m["hx"] = sb("hx", [P, TILES, FX])
    m["hs"] = sb("hs", [P, 2, TILES, FX], F32R)
    m["w"] = sb("w_sb", [128, 4, 2, F])
    m["arena"] = sb("arena", [128, ARENA])
    m["table"] = sb("table", [128, 3, TILES, TILES])
    m["nv"] = sb("nv_sb", [P, TILES])
    m["ident"] = sb("ident", [128, 128])
    m["identb"] = sb("identb", [128, 128], BF16)
    m["ones"] = sb("ones", [128, 128])
    m["earlier"] = sb("earlier", [128, 128], BF16)
    m["one_up"] = sb("one_up", [128, 128])
    m["row"] = sb("row", [128, 1])
    m["minus_half"] = sb("minus_half", [P, 1])
    m["starts"] = sb("starts", [1, 32], I32)
    m["flags"] = sb("flags", [1, 2], I32)
    m["bias0"] = sb("bias0", [P, F])
    m["bias2"] = sb("bias2", [P, F])
    m["attn"] = sb("attn", [P, 4, F])
    m["hl"] = sb("hl", [P, TILES, HEADS])
    m["hr"] = sb("hr", [P, TILES, HEADS])
    m["logit"] = sb("logit", [P, TILES, 3, 12], BF16)
    m["logit_r"] = sb("logit_r", [P, TILES, 3, HEADS], F32R)
    return m


def load_and_starts(nc, m, d):
    with ExitStack() as ctx:
        loaded = ctx.enter_context(nc.semaphore("loaded"))
        dst_in = ctx.enter_context(nc.semaphore("dst_in"))
        iotas = ctx.enter_context(nc.semaphore("iotas"))
        made = ctx.enter_context(nc.semaphore("made"))
        summed = ctx.enter_context(nc.semaphore("summed"))
        dst_i = ctx.enter_context(nc.sbuf_tensor("dst_i", [P, GEN], I32))
        dst_f = m["arena"][0:P, 0:GEN]
        less = m["arena"][0:P, GEN:2 * GEN]
        below = m["arena"][0:P, 2 * GEN:2 * GEN + TILES]
        grid = ctx.enter_context(nc.sbuf_tensor("grid", [128, 128], I32))
        rowi = ctx.enter_context(nc.sbuf_tensor("rowi", [128, 1], I32))
        first = ctx.enter_context(nc.sbuf_tensor("first", [1, TILES], F32))
        total = ctx.enter_context(nc.psum_tensor("total", [1, TILES], F32))
        block = ctx.enter_context(nc.Block())
        loads = 7 + 4

        @block.sync
        def _(sync):
            sync.dma_start(dst_i[:, :], d["dst"].rearrange("(p c) -> p c", c=GEN)).then_inc(dst_in, 16)
            sync.dma_start(m["x"][:, :, :], d["x"].rearrange("(t p) f -> p t f", p=P)).then_inc(loaded, 16)
            for n, name in enumerate(("w0", "w1", "w2", "w3")):
                sync.dma_start(m["w"][:, n, :, :], d[name].rearrange("(c k) n -> k c n", k=128)).then_inc(loaded, 16)
            sync.dma_start(m["bias0"][:, :], d["bias0"].partition_broadcast(P)).then_inc(loaded, 16)
            sync.dma_start(m["bias2"][:, :], d["bias2"].partition_broadcast(P)).then_inc(loaded, 16)
            for n, name in enumerate(("al1", "ar1", "al3", "ar3")):
                sync.dma_start(m["attn"][:, n, :], d[name].partition_broadcast(P)).then_inc(loaded, 16)
            with nc.allow_non_contiguous_dma(reason="12.5 KB, once"):
                sync.dma_start(m["nv"][:, :], d["nv"].rearrange("(t p) -> p t", p=P)).then_inc(loaded, 16)
            sync.wait_ge(loaded, 16 * 12)

        @block.gpsimd
        def _(pool):
            pool.iota(grid[:, :], [[1, 128]], base=1, channel_multiplier=0).then_inc(iotas, 1)
            pool.iota(rowi[:, :], [[1, 1]], base=1, channel_multiplier=1).then_inc(iotas, 1)
            pool.memset(m["ones"][:, :], 1.0).then_inc(iotas, 1)
            pool.memset(m["minus_half"][:, :], -0.5)

        @block.vector
        def _(vec):
            vec.wait_ge(iotas, 3)
            vec.tensor_copy(m["one_up"][:, :], grid[:, :]).then_inc(made, 1)
            vec.tensor_copy(m["row"][:, :], rowi[:, :]).then_inc(made, 1)
            vec.wait_ge(made, 2)
            vec.tensor_scalar(m["ident"][:, :], m["one_up"][:, :], m["row"][:, :], None, ALU.is_equal).then_inc(made, 1)
            vec.tensor_scalar(m["identb"][:, :], m["one_up"][:, :], m["row"][:, :], None, ALU.is_equal).then_inc(made, 1)
            vec.tensor_scalar(m["earlier"][:, :], m["one_up"][:, :], m["row"][:, :], None, ALU.is_gt).then_inc(made, 1)
            vec.wait_ge(dst_in, 16)
            vec.tensor_copy(dst_f, dst_i[:, :]).then_inc(made, 1)
            for j in range(TILES):
                vec.wait_ge(made, 6 + j)
                vec.tensor_scalar(less, dst_f, float(P * j), None, ALU.is_lt, ALU.add,
                                  accum_out=below[:, j:j + 1]).then_inc(made, 1)
            vec.wait_ge(summed, 1)
            vec.tensor_scalar(first[:, :], total[:, :], float(E - WIN), None, ALU.min).then_inc(made, 1)
            vec.wait_ge(made, 7 + TILES)
            vec.tensor_copy(m["starts"][:, 0:TILES], first[:, :]).then_inc(made, 1)

        @block.tensor
        def _(pe):
            pe.wait_ge(made, 6 + TILES)
            pe.matmul(total[:, :], m["ones"][0:P, 0:1], below, start=True, stop=True).then_inc(summed, 1)


def in_pairs(eng, body):
    with eng.Fori(0, TILES // 2) as pair:
        body(2 * pair, 0, True)
        body(2 * pair + 1, 1, True)
    body(TILES - 1, 0, False)


def with_last(eng, body):
    body(0, 0, None, True)
    with eng.Fori(0, TILES // 2 - 1) as pair:
        body(2 * pair + 1, 1, 2 * pair, True)
        body(2 * pair + 2, 0, 2 * pair + 1, True)
    body(TILES - 2, 1, TILES - 3, True)
    body(TILES - 1, 0, TILES - 2, False)


def build_table(nc, m, d):
    with ExitStack() as ctx:
        def sem(name):
            return ctx.enter_context(nc.semaphore(name))

        def sb(name, shape, dt=F32):
            return ctx.enter_context(nc.sbuf_tensor(name, shape, dt))

        win_in = sem("win_in")
        weights_in = sem("weights_in")
        iotas = sem("iotas")
        calc = sem("calc")
        step = sem("step")
        tile_hot = sem("tile_hot")
        counts_ready = sem("counts_ready")
        base_ready = sem("base_ready")
        rank_hot = sem("rank_hot")
        pay_ready = sem("pay_ready")
        moved = sem("moved")
        kept = sem("kept")
        turned = sem("turned")
        rows_out = sem("rows_out")
        stored = sem("stored")
        src_i = sb("src_w", [128, TILES, CH], I32)
        dst_i = sb("dst_w", [128, TILES, CH], I32)
        starts_i = sb("starts_i", [128, TILES], I32)
        starts_f = sb("starts_f", [128, TILES])
        values = sb("values", [128, PAY, TILES, CH], BF16)
        weight = sb("weight", [128, TILES, CH])
        tile_of = sb("tile_of", [128, TILES, CH])
        t1, t2, t3 = (sb(f"t{n}", [128, TILES, CH]) for n in (1, 2, 3))
        raw = sb("raw", [128, PAY, TILES, TILES], BF16)
        placed = sb("placed", [128, 1])
        all_in = sb("all_in", [1, 1])
        spaces = [m["arena"], sb("more", [128, 4100])]
        taken = [0, 0]

        def take(n, dt=F32):
            words = n if dt == F32 else n // 2
            k = 0 if taken[0] + words <= ARENA else 1
            taken[k] += words
            part = spaces[k][:, taken[k] - words:taken[k]]
            return part if dt == F32 else part.bitcast(dt)

        def by_tile(t):
            return t.rearrange("p (a c) -> p a c", c=CH)

        hot = [take(TILES * CH) for _ in range(2)]
        running = [take(TILES * CH) for _ in range(2)]
        keep, rank_of = take(TILES * CH), take(TILES * CH)
        rank = take(CH)
        counts = take(32, BF16)
        ranks = [take(CH * RANKS, BF16).rearrange("p (c r) -> p c r", r=RANKS) for _ in range(2)]
        pay = [take(CH * PAY * TILES, BF16).rearrange("p (c k a) -> p c k a", c=CH, k=PAY) for _ in range(2)]
        scratch = take(TILES * TILES)
        rows = take(10 * RANKS, BF16).rearrange("p (k r) -> p k r", r=RANKS)
        base = ctx.enter_context(nc.psum_tensor("base", [128, 512], F32))
        out = [ctx.enter_context(nc.psum_tensor(f"buckets{i}", [128, 512], F32)) for i in range(2)]
        turn = ctx.enter_context(nc.psum_tensor("turn", [128, 2, 1024], BF16))
        block = ctx.enter_context(nc.Block())

        def load_windows(eng, tile, name, landed):
            with eng.Fori(0, TILES) as j:
                start = eng.value_load(m["starts"][0:1, at(j)], min_val=0, max_val=E - WIN)
                eng.dma_start(tile[:, at(j), :],
                              d[name][bass.ds(start, WIN)].rearrange("(p o c) -> p o c", p=128, o=1)
                              ).then_inc(landed, 16)

        @block.sync
        def _(sync):
            load_windows(sync, src_i, "src", win_in)
            sync.wait_ge(rows_out, 2)
            for k in range(2):
                sync.dma_start(d["rows"][k].rearrange("(c p) r -> p c r", p=P),
                               rows[0:P, 5 * k:5 * k + 5, :]).then_inc(stored, 16)
            sync.wait_ge(stored, 32)

        @block.gpsimd
        def _(pool):
            pool.iota(starts_i[:, :], [[P, TILES]], base=-1, channel_multiplier=0).then_inc(iotas, 1)
            pool.memset(keep, 1.0).then_inc(iotas, 1)
            pool.wait_ge(iotas, 2)
            pool.memset(by_tile(keep)[:, :, 0:1], 0.0).then_inc(iotas, 1)
            load_windows(pool, weight, "ew", weights_in)
            pool.wait_ge(calc, 14)

            def payload(j, slot, more):
                pool.wait_ge(tile_hot, j + 1)
                pool.wait_ge(moved, CREDIT + j - 1)
                pool.tensor_tensor(
                    pay[slot],
                    by_tile(hot[slot]).rearrange("p a (c o) -> p c o a", o=1).to_broadcast([128, CH, PAY, TILES]),
                    values[:, :, at(j), :].rearrange("p k o (c b) -> p (o c) k b", b=1).to_broadcast(
                        [128, CH, PAY, TILES]), ALU.mult).then_inc(pay_ready, 1)

            in_pairs(pool, payload)

        @block.vector
        def _(vec):
            n = Count()
            vec.wait_ge(win_in, 16 * 2 * TILES)
            vec.wait_ge(weights_in, 16 * TILES)
            vec.wait_ge(iotas, 3)
            vec.tensor_copy(t1[:, :, :], src_i[:, :, :]).then_inc(calc, n.one())
            vec.tensor_copy(t2[:, :, :], dst_i[:, :, :]).then_inc(calc, n.one())
            vec.tensor_copy(starts_f[:, :], starts_i[:, :]).then_inc(calc, n.one())
            vec.tensor_copy(values[:, 2, :, :], weight[:, :, :]).then_inc(calc, n.one())
            vec.wait_ge(calc, n.now())
            vec.tensor_tensor(t2[:, :, :], t2[:, :, :],
                              starts_f[:, :].rearrange("p (j o) -> p j o", o=1).to_broadcast([128, TILES, CH]),
                              ALU.subtract).then_inc(calc, n.one())
            vec.tensor_scalar(t3[:, :, :], t1[:, :, :], 1.0 / P, 0.5 / P - 0.5, ALU.mult, ALU.add
                              ).then_inc(calc, n.one())
            vec.tensor_tensor(weight[:, :, :], weight[:, :, :], values[:, 2, :, :], ALU.subtract
                              ).then_inc(calc, n.one())
            vec.wait_ge(calc, n.now())
            vec.tensor_scalar(t3[:, :, :], t3[:, :, :], MAGIC, None, ALU.add).then_inc(calc, n.one())
            vec.tensor_copy(values[:, 1, :, :], t2[:, :, :]).then_inc(calc, n.one())
            vec.tensor_copy(values[:, 3, :, :], weight[:, :, :]).then_inc(calc, n.one())
            vec.wait_ge(calc, n.now())
            vec.tensor_scalar(t3[:, :, :], t3[:, :, :], MAGIC, None, ALU.subtract).then_inc(calc, n.one())
            vec.tensor_tensor(values[:, 4, :, :], weight[:, :, :], values[:, 3, :, :], ALU.subtract
                              ).then_inc(calc, n.one())
            vec.wait_ge(calc, n.now())
            vec.scalar_tensor_tensor(t1[:, :, :], t3[:, :, :], -float(P), t1[:, :, :], ALU.mult, ALU.add
                                     ).then_inc(calc, n.one())
            vec.wait_ge(calc, n.now())
            vec.tensor_scalar(values[:, 0, :, :], t1[:, :, :], 1.0, None, ALU.add).then_inc(calc, n.one())
            vec.wait_ge(calc, n.now())
            vec.tensor_scalar(t1[:, :, :], t2[:, :, :], 1.0, None, ALU.is_ge).then_inc(calc, n.one())
            vec.wait_ge(calc, n.now())
            vec.scalar_tensor_tensor(t1[:, :, :], t2[:, :, :], float(P), t1[:, :, :], ALU.is_le, ALU.mult
                                     ).then_inc(calc, n.one())
            vec.wait_ge(calc, n.now())
            vec.scalar_tensor_tensor(tile_of[:, :, :], t3[:, :, :], 1.0, t1[:, :, :], ALU.add, ALU.mult
                                     ).then_inc(calc, n.one())
            vec.wait_ge(calc, n.now())
            vec.sem_inc(moved, CREDIT)
            vec.sem_inc(kept, CREDIT)

            def source_tiles(j, slot):
                vec.wait_ge(pay_ready, CREDIT + j - 1)
                vec.tensor_tensor(
                    by_tile(hot[slot]), tile_of[:, at(j), :].to_broadcast([128, TILES, CH]),
                    m["one_up"][:, 0:TILES].rearrange("p (a o) -> p a o", o=1).to_broadcast([128, TILES, CH]),
                    ALU.is_equal).then_inc(tile_hot, 1)

            def scan(j, slot):
                vec.wait_ge(tile_hot, j + 1)
                vec.tensor_tensor_scan(running[slot], keep, hot[slot], 0.0, ALU.mult, ALU.add).then_inc(step, 1)

            def count(slot, scanned):
                vec.wait_ge(step, scanned)
                vec.tensor_copy(counts[:, 0:TILES], by_tile(running[slot])[:, :, CH - 1]).then_inc(counts_ready, 1)

            def sort_tile(j, slot, more):
                steps = 4 * j + 1
                if more:
                    source_tiles(j + 1, 1 - slot)
                vec.wait_ge(base_ready, j + 1)
                vec.tensor_tensor(
                    by_tile(rank_of), by_tile(running[slot]),
                    base[:, 0:TILES].rearrange("p (a o) -> p a o", o=1).to_broadcast([128, TILES, CH]), ALU.add
                    ).then_inc(step, 1)
                if more:
                    scan(j + 1, 1 - slot)
                vec.wait_ge(step, steps + 1)
                vec.tensor_tensor(rank_of, rank_of, hot[slot], ALU.mult).then_inc(step, 1)
                if more:
                    count(1 - slot, steps + 2)
                vec.wait_ge(step, steps + (3 if more else 2))
                vec.tensor_reduce(rank, by_tile(rank_of).rearrange("p a c -> p c a"), AX.X, ALU.add
                                  ).then_inc(step, 1)
                vec.wait_ge(step, steps + (4 if more else 3))
                vec.wait_ge(moved, CREDIT + j - 1)
                vec.tensor_tensor(
                    ranks[slot], rank.rearrange("p (c o) -> p c o", o=1).to_broadcast([128, CH, RANKS]),
                    m["one_up"][:, :].rearrange("p (o r) -> p o r", o=1).to_broadcast([128, CH, RANKS]),
                    ALU.is_equal).then_inc(rank_hot, 1)

            vec.sem_inc(pay_ready, CREDIT)
            source_tiles(0, 0)
            scan(0, 0)
            count(0, 1)
            in_pairs(vec, sort_tile)

            vec.wait_ge(kept, CREDIT + TILES)
            vec.tensor_copy(m["table"][:, 0:2, :, :], raw[:, 0:2, :, :]).then_inc(calc, n.one())
            vec.tensor_tensor(m["table"][:, 2, :, :], raw[:, 3, :, :], raw[:, 4, :, :], ALU.add
                              ).then_inc(calc, n.one())
            vec.wait_ge(calc, n.now())
            vec.tensor_tensor(m["table"][:, 2, :, :], m["table"][:, 2, :, :], raw[:, 2, :, :], ALU.add
                              ).then_inc(calc, n.one())
            vec.tensor_scalar(scratch, m["table"][:, 1, :, :].rearrange("p a j -> p (a j)"), 0.0, None,
                              ALU.is_gt, ALU.add, accum_out=placed[:, :]).then_inc(calc, n.one())
            vec.wait_ge(base_ready, TILES + 1)
            vec.tensor_scalar(all_in[:, :], base[0:1, 0:1], float(E), None, ALU.is_equal).then_inc(calc, n.one())
            vec.wait_ge(calc, n.now())
            vec.tensor_copy(m["flags"][:, 0:1], all_in[:, :]).then_inc(calc, n.one())

        @block.tensor
        def _(pe):
            def before(j):
                pe.wait_ge(counts_ready, j + 1)
                pe.matmul(base[:, 0:TILES], m["earlier"][:, :], counts[:, 0:TILES], start=True, stop=True
                          ).then_inc(base_ready, 1)

            def move(j, slot, more):
                if more:
                    before(j + 1)
                pe.wait_ge(rank_hot, j + 1)
                pe.wait_ge(pay_ready, CREDIT + j + 1)
                pe.wait_ge(kept, CREDIT + j - 1)
                for c in range(CH):
                    last = pe.matmul(out[slot][:, 0:PAY * TILES], ranks[slot][:, c, :],
                                     pay[slot][:, c, :, :].rearrange("p k a -> p (k a)"),
                                     start=c == 0, stop=c == CH - 1)
                last.then_inc(moved, 1)

            before(0)
            in_pairs(pe, move)
            pe.wait_ge(calc, 21)
            pe.matmul(base[0:1, 0:1], m["ones"][:, 0:1], placed[:, :], start=True, stop=True).then_inc(base_ready, 1)
            for k in range(2):
                for c in range(5):
                    last = pe.transpose(turn[0:P, k, c * RANKS:(c + 1) * RANKS],
                                        raw[:, k, 5 * c:5 * c + 5, :].rearrange("p a j -> p (a j)"),
                                        m["identb"][:, :])
                last.then_inc(turned, 1)

        @block.scalar
        def _(act):
            def keep_tile(j, slot, more):
                act.wait_ge(moved, CREDIT + j + 1)
                act.copy(raw[:, :, :, at(j)].rearrange("p k a o -> p k (a o)"),
                         out[slot][:, 0:PAY * TILES].rearrange("p (k a) -> p k a", k=PAY)).then_inc(kept, 1)

            load_windows(act, dst_i, "dst", win_in)
            in_pairs(act, keep_tile)
            for k in range(2):
                act.wait_ge(turned, k + 1)
                act.copy(rows[0:P, 5 * k:5 * k + 5, :],
                         turn[0:P, k, 0:5 * RANKS].rearrange("p (c r) -> p c r", r=RANKS)).then_inc(rows_out, 1)


def project(nc, m, weight, layer, split, attn=None, d=None):
    with ExitStack() as ctx:
        def sem(name):
            return ctx.enter_context(nc.semaphore(f"{name}_p{layer}"))

        def sb(name, shape, dt=F32):
            return [ctx.enter_context(nc.sbuf_tensor(f"{name}_p{layer}_{i}", shape, dt)) for i in range(2)]

        staged = sem("staged")
        turned = sem("turned")
        turned_kept = sem("turned_kept")
        product = sem("product")
        copied = sem("copied")
        step = sem("step")
        xs, xt = sb("xs", [P, F]), sb("xt", [128, 2, P])
        by_l, by_r = sb("by_l", [P, F]), sb("by_r", [P, F])
        pt = [ctx.enter_context(nc.psum_tensor(f"pt{layer}_{i}", [128, 512], F32)) for i in range(2)]
        ph = [ctx.enter_context(nc.psum_tensor(f"ph{layer}_{i}", [P, 512], F32)) for i in range(2)]
        hxv = m["hx"][:, :, :].rearrange("p t (h e) -> p t h e", e=HX)
        hsv = m["hs"][:, :, :, :].rearrange("p s t (h e) -> p s t h e", e=HX)
        copies = 2 if split else 1
        steps = bool(split) + 4 * (attn is not None)

        def heads(t):
            return t.rearrange("p (h d) -> p h d", d=HD)

        def row(t, j):
            return t[:, at(j), :, 0:HD].rearrange("p o h d -> p (o h) d")

        block = ctx.enter_context(nc.Block())

        if d:
            stored = sem("stored")

            @block.sync
            def _(sync):
                def store(j, slot, more):
                    sync.wait_ge(step, steps * j + steps)
                    sync.dma_start(d["targets"][bass.ds(P * j, P), :], m["hx"][:, at(j), :].rearrange(
                        "p o e -> p (o e)")).then_inc(stored, 16)
                    with nc.allow_non_contiguous_dma(reason="2 KB"):
                        sync.dma_start(d["sources"][bass.ds(P * j, P), :], m["hl"][:, at(j), :].rearrange(
                            "p o h -> p (o h)")).then_inc(stored, 16)

                in_pairs(sync, store)
                sync.wait_ge(stored, 2 * 16 * TILES)

        @block.gpsimd
        def _(pool):
            if split:
                pool.memset(hxv[:, :, :, HD], 1.0)
                pool.memset(hsv[:, 0, :, :, HD].bitcast(F32), 1.0)
                pool.memset(hsv[:, 1, :, :, HD].bitcast(F32), 0.0)

            def tile(j, slot, more):
                pool.wait_ge(turned, CREDIT + j - 1)
                pool.tensor_copy(xs[slot][:, :], m["x"][:, at(j), :].rearrange("p o f -> p (o f)")
                                 ).then_inc(staged, 1)

            pool.sem_inc(turned_kept, CREDIT)
            in_pairs(pool, tile)

        @block.tensor
        def _(pe):
            def turn(j, slot):
                pe.wait_ge(staged, j + 1)
                pe.wait_ge(turned_kept, CREDIT + j - 1)
                for c in range(2):
                    last = pe.transpose(pt[slot][:, c * 128:c * 128 + P], xs[slot][:, c * 128:(c + 1) * 128],
                                        m["ident"][0:P, 0:P])
                last.then_inc(turned, 1)

            def tile(j, slot, more):
                if more:
                    turn(j + 1, 1 - slot)
                pe.wait_ge(turned_kept, CREDIT + j + 1)
                pe.wait_ge(copied, copies * j + CREDIT - copies)
                for c in range(2):
                    last = pe.matmul(ph[slot][:, 0:F], xt[slot][:, c, :], m["w"][:, weight, c, :],
                                     start=c == 0, stop=c == 1)
                last.then_inc(product, 1)

            pe.sem_inc(turned, CREDIT)
            turn(0, 0)
            in_pairs(pe, tile)

        @block.scalar
        def _(act):
            def keep(j, slot):
                act.wait_ge(turned, CREDIT + j + 1)
                act.wait_ge(product, CREDIT + j - 1)
                act.copy(xt[slot][:, :, :], pt[slot][:, 0:256].rearrange("p (c n) -> p c n", c=2)[:, :, 0:P]
                         ).then_inc(turned_kept, 1)

            def tile(j, slot, more):
                if more:
                    keep(j + 1, 1 - slot)
                act.wait_ge(product, CREDIT + j + 1)
                if split:
                    act.copy(row(hsv[:, 0], j), heads(ph[slot][:, 0:F])).then_inc(copied, 1)
                act.copy(row(hxv, j), heads(ph[slot][:, 0:F])).then_inc(copied, 1)

            act.sem_inc(product, CREDIT)
            keep(0, 0)
            in_pairs(act, tile)

        @block.vector
        def _(vec):
            def tile(j, slot, more):
                s = Count(steps * j)
                h = row(hxv, j)
                vec.wait_ge(copied, CREDIT + copies * (j + 1))
                if attn is not None:
                    for n, by in enumerate((by_l, by_r)):
                        vec.tensor_tensor(heads(by[slot][:, :]), h, heads(m["attn"][:, attn + n, :]), ALU.mult
                                          ).then_inc(step, s.one())
                if split:
                    vec.tensor_tensor(row(hsv[:, 1], j), h, row(hsv[:, 0], j).bitcast(F32), ALU.subtract
                                      ).then_inc(step, s.one())
                if attn is not None:
                    vec.wait_ge(step, s.now())
                    right = hxv[:, at(j), :, HD] if d else m["hr"][:, at(j), :]
                    for by, into in ((by_l, m["hl"][:, at(j), :]), (by_r, right)):
                        vec.tensor_reduce(into.rearrange("p o h -> p (o h)"), heads(by[slot][:, :]), AX.X, ALU.add
                                          ).then_inc(step, s.one())

            vec.sem_inc(copied, CREDIT)
            if steps:
                in_pairs(vec, tile)


def attention_inputs(nc, m):
    with ExitStack() as ctx:
        def sb(name, shape, dt=F32):
            return ctx.enter_context(nc.sbuf_tensor(name, shape, dt))

        step = ctx.enter_context(nc.semaphore("step_a"))
        done = ctx.enter_context(nc.semaphore("done_a"))
        ends = sb("ends", [P, 8])
        top = sb("top", [8, 1])
        spread_out = sb("spread_out", [8, 8])
        of_all = sb("of_all", [P, 8])
        cat = sb("cat", [P, TILES, 12])
        rest = sb("rest_a", [P, TILES, 12])
        small = sb("small", [1, 4])
        flag = sb("flag_f", [1, 2])
        pa = ctx.enter_context(nc.psum_tensor("pa", [128, 512], F32))
        pb = ctx.enter_context(nc.psum_tensor("pb", [128, 512], F32))
        block = ctx.enter_context(nc.Block())

        @block.tensor
        def _(pe):
            pe.wait_ge(step, 3)
            pe.transpose(pa[0:8, 0:P], ends[:, :], m["ident"][0:P, 0:P]).then_inc(done, 1)
            pe.wait_ge(step, 7)
            pe.matmul(pb[0:P, 0:8], m["ones"][0:8, 0:P], spread_out[:, :], start=True, stop=True).then_inc(done, 1)

        @block.vector
        def _(vec):
            n = Count()
            by_head = m["hr"][:, :, :].rearrange("p t h -> p h t")
            logits = cat[:, :, 4:8]
            vec.tensor_reduce(ends[:, 0:4], by_head, AX.X, ALU.max).then_inc(step, n.one())
            vec.tensor_reduce(ends[:, 4:8], by_head, AX.X, ALU.min).then_inc(step, n.one())
            vec.wait_ge(step, n.now())
            vec.tensor_scalar(ends[:, 4:8], ends[:, 4:8], -1.0, None, ALU.mult).then_inc(step, n.one())
            vec.tensor_copy(cat[:, :, 0:4], m["hl"][:, :, :]).then_inc(step, n.one())
            vec.tensor_copy(cat[:, :, 8:12], m["hr"][:, :, :]).then_inc(step, n.one())
            vec.wait_ge(done, 1)
            vec.tensor_reduce(top[:, :], pa[0:8, 0:P], AX.X, ALU.max).then_inc(step, n.one())
            vec.wait_ge(step, n.now())
            vec.tensor_scalar(spread_out[:, :], m["ident"][0:8, 0:8], top[:, :], None, ALU.mult
                              ).then_inc(step, n.one())
            vec.wait_ge(done, 2)
            vec.tensor_copy(of_all[:, :], pb[0:P, 0:8]).then_inc(step, n.one())
            vec.wait_ge(step, n.now())
            vec.tensor_tensor(logits, m["hl"][:, :, :],
                              of_all[:, 0:4].rearrange("p (o h) -> p o h", o=1).to_broadcast([P, TILES, HEADS]),
                              ALU.add).then_inc(step, n.one())
            vec.tensor_tensor(small[:, :], of_all[0:1, 0:4], of_all[0:1, 4:8], ALU.add).then_inc(step, n.one())
            vec.tensor_copy(flag[:, 0:1], m["flags"][:, 0:1]).then_inc(step, n.one())
            vec.wait_ge(step, n.now())
            vec.scalar_tensor_tensor(logits, logits, 0.2, logits, ALU.mult, ALU.max).then_inc(step, n.one())
            vec.tensor_reduce(flag[:, 1:2], small[:, :], AX.X, ALU.max).then_inc(step, n.one())
            vec.wait_ge(step, n.now())
            vec.tensor_copy(m["logit"][:, :, 0, :], cat[:, :, :]).then_inc(step, n.one())
            vec.scalar_tensor_tensor(flag[:, 1:2], flag[:, 1:2], SPREAD, flag[:, 0:1], ALU.is_le, ALU.mult
                                     ).then_inc(step, n.one())
            vec.wait_ge(step, n.now())
            vec.tensor_tensor(rest[:, :, :], cat[:, :, :], m["logit"][:, :, 0, :], ALU.subtract
                              ).then_inc(step, n.one())
            vec.tensor_copy(m["flags"][:, 1:2], flag[:, 1:2]).then_inc(step, n.one())
            vec.wait_ge(step, n.now())
            vec.tensor_copy(m["logit"][:, :, 1, :], rest[:, :, :]).then_inc(step, n.one())
            vec.wait_ge(step, n.now())
            vec.tensor_tensor(m["logit"][:, :, 2, :], rest[:, :, :], m["logit"][:, :, 1, :], ALU.subtract
                              ).then_inc(step, n.one())
            vec.wait_ge(step, n.now())
            vec.tensor_copy(m["logit_r"][:, :, :, :], m["logit"][:, :, :, 8:12]).then_inc(step, n.one())


def split_edges(nc, m):
    with ExitStack() as ctx:
        filled = ctx.enter_context(nc.semaphore("filled_s"))
        firsts = ctx.enter_context(nc.semaphore("firsts"))
        block = ctx.enter_context(nc.Block())
        parts = [slice(5 * g, 5 * g + 5) for g in range(5)]

        @block.gpsimd
        def _(pool):
            pool.tensor_copy(m["hx"][:, :, :].rearrange("p t (h e) -> p t h e", e=HX)[:, :, :, HD],
                             m["nv"][:, :].rearrange("p (t o) -> p t o", o=1).to_broadcast([P, TILES, HEADS])
                             ).then_inc(filled, 1)

        @block.scalar
        def _(act):
            act.wait_ge(filled, 1)
            for part in parts:
                act.copy(m["hs"][:, 0, part, :], m["hx"][:, part, :]).then_inc(firsts, 1)

        @block.vector
        def _(vec):
            vec.wait_ge(filled, 1)
            for g, part in enumerate(parts):
                vec.wait_ge(firsts, g + 1)
                vec.tensor_tensor(m["hs"][:, 1, part, :], m["hx"][:, part, :], m["hs"][:, 0, part, :].bitcast(F32),
                                  ALU.subtract)


class Finish:

    PARTS = {0: 6, 1: 8, 2: 3, 3: 9}

    def __init__(self, nc, ctx, m, kind, psum_sums):
        def sb(name, shape):
            return ctx.enter_context(nc.sbuf_tensor(f"{name}_f{kind}", shape, F32))

        self.m, self.kind, self.sums, self.parts = m, kind, psum_sums, self.PARTS[kind]
        self.step = ctx.enter_context(nc.semaphore(f"step_f{kind}"))
        if kind != 2:
            self.variance = ctx.enter_context(nc.semaphore(f"variance_f{kind}"))
            self.rooted = ctx.enter_context(nc.semaphore(f"rooted_f{kind}"))
        self.sums_used = ctx.enter_context(nc.semaphore(f"sums_used_f{kind}"))
        self.new, self.out = (m["w"][0:P, 0, c, :] if kind else sb(f"new{c}", [P, F])[:, :] for c in range(2))
        self.small, self.stats, self.mean = sb("small", [P, 8]), sb("stats", [P, 6]), sb("mean", [P, 2])
        self.inv = sb("inv", [P, 1])

    def root(self, pool, j):
        pool.wait_ge(self.variance, j + 1)
        pool.tensor_tensor(self.inv[:, :], self.mean[:, 1:2], self.m["minus_half"][:, :], ALU.pow
                           ).then_inc(self.rooted, 1)

    def start(self, vec):
        vec.sem_inc(self.step, CREDIT)
        vec.sem_inc(self.sums_used, CREDIT)

    def normalize(self, vec, k, j):
        m, step = self.m, self.step
        if k == 0:
            vec.bn_stats(self.stats[:, :], self.new).then_inc(step, 1)
        if k == 1:
            vec.drain()
            vec.bn_aggr(self.mean[:, :], self.stats[:, :]).then_inc(step, 1)
        if k == 2:
            vec.tensor_scalar(self.mean[:, 1:2], self.mean[:, 1:2], EPS, None, ALU.add).then_inc(self.variance, 1)
            vec.sem_inc(step, 1)
        if k == 3:
            vec.wait_ge(self.rooted, j + 1)
            vec.tensor_scalar(m["x"][:, at(j), :].rearrange("p o f -> p (o f)"), self.new, self.mean[:, 0:1],
                              self.inv[:, :], ALU.subtract, ALU.mult).then_inc(step, 1)

    def part(self, vec, k, j, slot):
        m, step, small = self.m, self.step, self.small
        sums = self.sums[slot]
        heads = sums[:, 0:FX].rearrange("p (h e) -> p h e", e=HX)
        features, degree = heads[:, :, 0:HD], heads[:, 0, HD:HX]
        new = self.new.rearrange("p (h d) -> p h d", d=HD)
        out = self.out.rearrange("p (h d) -> p h d", d=HD)
        x = m["x"][:, at(j), :].rearrange("p o f -> p (o f)")
        x_heads = m["x"][:, at(j), :].rearrange("p o (h d) -> p (o h) d", d=HD)
        if self.kind == 2 or k != self.parts - 3:
            vec.wait_ge(step, self.parts * j + (CREDIT + k))
        if self.kind == 0:
            if k == 0:
                vec.tensor_tensor(out, features, m["bias0"][:, :].rearrange("p (h d) -> p h d", d=HD), ALU.add
                                  ).then_inc(step, 1)
            if k == 1:
                vec.sem_inc(self.sums_used, 1)
                vec.scalar_tensor_tensor(self.new, self.out, 0.0, x, ALU.max, ALU.add).then_inc(step, 1)
        if self.kind == 1:
            if k == 0:
                vec.tensor_scalar(small[:, 0:4], heads[:, :, HD], 1e-30, None, ALU.max).then_inc(step, 1)
            if k == 1:
                vec.reciprocal(small[:, 4:8], small[:, 0:4]).then_inc(step, 1)
            if k == 2:
                vec.tensor_tensor(out, features,
                                  small[:, 4:8].rearrange("p (h o) -> p h o", o=1).to_broadcast([P, HEADS, HD]),
                                  ALU.mult).then_inc(step, 1)
            if k == 3:
                vec.sem_inc(self.sums_used, 1)
                vec.tensor_tensor(self.new, self.out, x, ALU.add).then_inc(step, 1)
        if self.kind == 2:
            if k == 0:
                vec.tensor_scalar(small[:, 0:1], degree, 1.0, None, ALU.max).then_inc(step, 1)
            if k == 1:
                vec.reciprocal(small[:, 1:2], small[:, 0:1]).then_inc(step, 1)
            if k == 2:
                vec.tensor_scalar(m["hx"][:, at(j), :].rearrange("p o (h e) -> p (o h) e", e=HX)[:, :, 0:HD],
                                  features, small[:, 1:2], None, ALU.mult).then_inc(self.sums_used, 1)
                vec.sem_inc(step, 1)
        if self.kind == 3:
            if k == 0:
                vec.tensor_scalar(small[:, 0:1], degree, 0.0, None, ALU.is_le).then_inc(step, 1)
            if k == 1:
                vec.scalar_tensor_tensor(small[:, 1:2], degree, 0.0, small[:, 0:1], ALU.max, ALU.add
                                         ).then_inc(step, 1)
            if k == 2:
                vec.reciprocal(small[:, 2:3], small[:, 1:2]).then_inc(step, 1)
            if k == 3:
                vec.scalar_tensor_tensor(small[:, 3:4], degree, 0.0, small[:, 2:3], ALU.is_gt, ALU.mult
                                         ).then_inc(step, 1)
            if k == 4:
                vec.scalar_tensor_tensor(new, features, small[:, 3:4], x_heads, ALU.mult, ALU.add).then_inc(step, 1)
        if self.kind != 2 and k >= self.parts - 4:
            if self.kind == 3 and k == 5:
                vec.sem_inc(self.sums_used, 1)
            self.normalize(vec, k - (self.parts - 4), j)

    def tile(self, vec, j, slot):
        for k in range(self.parts):
            self.part(vec, k, j, slot)


def fast(eng, m, n):
    return eng.If(eng.value_load(m["flags"][0:1, n:n + 1], min_val=0, max_val=1) == 1)


class General:

    def __init__(self, nc, ctx, m, d, kind, sums, fin, bank=None):
        self.nc, self.m, self.d, self.kind, self.sums, self.fin, self.bank = nc, m, d, kind, sums[0], fin, bank
        taken = [0]

        def take(n):
            taken[0] += n
            return m["arena"][0:P, taken[0] - n:taken[0]]

        def sem(name):
            return ctx.enter_context(nc.semaphore(f"{name}_g{kind}"))

        self.loaded = sem("loaded")
        self.ready = sem("ready")
        self.row_in = [sem(f"row_in{i}") for i in range(len(THIRDS))]
        self.message = sem("message")
        self.added = sem("added")
        self.step = sem("step")
        if kind == 1:
            self.edge_in = sem("edge_in")
            self.edge_read = sem("edge_read")
            self.apart = sem("apart")
            self.turned = sem("turned")
            self.best_in = sem("best_in")
            self.best_out = sem("best_out")
            self.top_in = sem("top_in")
            self.above = sem("above")
            self.weights = sem("weights")
        self.gather_index, self.sum_index, self.weight = take(GEN).bitcast(I32), take(GEN).bitcast(I32), take(GEN)
        self.local = take(GEN)
        self.coef = take(GEN * HEADS).rearrange("p (c h) -> p c h", h=HEADS)
        self.now = [take(1).bitcast(I32) for _ in range(2)]
        self.ends = [take(HEADS) for _ in range(2)]
        self.row, self.scaled, self.zero = take(FX), take(FX), take(FX)
        self.onehot, self.low = take(P), take(P)
        self.logits = take(P * HEADS).rearrange("p (h n) -> p h n", n=P)
        self.found = take(HEADS)
        self.best = take(TILES * HEADS).rearrange("p (t h) -> p t h", h=HEADS)

    def gpsimd(self, pool):
        m, d, nc = self.m, self.d, self.nc
        gather, add = ("src", "dst") if self.kind == 2 else ("dst", "src")
        pool.dma_start(self.gather_index, d[gather].rearrange("(p c) -> p c", c=GEN)).then_inc(self.loaded, 16)
        pool.dma_start(self.sum_index, d[add].rearrange("(p c) -> p c", c=GEN)).then_inc(self.loaded, 16)
        pool.dma_start(self.weight, d["ew"].rearrange("(p c) -> p c", c=GEN)).then_inc(self.loaded, 16)
        pool.dma_start(d["targets"].rearrange("(t p) e -> p t e", p=P), m["hx"][:, :, :]).then_inc(self.loaded, 16)
        if self.kind == 1:
            with nc.allow_non_contiguous_dma(reason="50 KB each, once"):
                for name, half in (("sources", "hl"), ("halves", "hr")):
                    pool.dma_start(d[name].rearrange("(t p) h -> p t h", p=P), m[half][:, :, :]
                                   ).then_inc(self.loaded, 16)
        pool.wait_ge(self.loaded, 96 if self.kind == 1 else 64)

        def index(k, column, c):
            return pool.tensor_copy(self.now[k], column[:, bass.ds(c, 1)])

        def rows(out, table, k):
            return pool.indirect_dma_start(out, None, d[table], bass.IndirectOffsetOnAxis(self.now[k], 0))

        if self.kind == 1:
            with pool.Fori(0, GEN) as c:
                pool.wait_ge(self.edge_read, CREDIT + c)
                index(0, self.sum_index, c)
                index(1, self.gather_index, c)
                pool.drain()
                rows(self.ends[0], "sources", 0).then_inc(self.edge_in, 16)
                rows(self.ends[1], "halves", 1).then_inc(self.edge_in, 16)
            pool.wait_ge(self.best_in, 1)
            with nc.allow_non_contiguous_dma(reason="50 KB, once"):
                pool.dma_start(d["tops"].rearrange("(t p) h -> p t h", p=P), self.best).then_inc(self.best_out, 16)
            pool.wait_ge(self.best_out, 16)
            with pool.Fori(0, GEN) as c:
                pool.wait_ge(self.weights, CREDIT + c)
                index(0, self.sum_index, c)
                pool.drain()
                rows(self.ends[0], "tops", 0).then_inc(self.top_in, 16)
        for third, (first, count) in enumerate(THIRDS):
            with pool.Fori(0, count) as t:
                with pool.Fori(0, GEN) as c:
                    pool.wait_ge(self.message, CREDIT + GEN * (t + first) + c)
                    index(1, self.gather_index, c)
                    pool.drain()
                    rows(self.row, "targets", 1).then_inc(self.row_in[third], 16)
                if self.kind != 2:
                    self.fin.root(pool, t + first)

    def vector(self, vec):
        m, kind, step = self.m, self.kind, self.step
        n = Count()
        vec.sem_inc(self.message, CREDIT)
        vec.sem_inc(self.added, CREDIT)
        if kind == 1:
            vec.sem_inc(self.edge_read, CREDIT)
            vec.sem_inc(self.weights, CREDIT)
            vec.sem_inc(self.turned, CREDIT)
        vec.wait_ge(self.loaded, 96 if kind == 1 else 64)
        vec.tensor_copy(self.local, self.sum_index).then_inc(self.ready, n.one())
        if kind == 0:
            vec.tensor_copy(self.coef, self.weight.rearrange("p (c o) -> p c o", o=1).to_broadcast([P, GEN, HEADS])
                            ).then_inc(self.ready, n.one())
        else:
            vec.memset(self.coef, 1.0).then_inc(self.ready, n.one())
        vec.memset(self.best, -3e38).then_inc(self.ready, n.one())
        vec.memset(self.zero, 0.0).then_inc(self.ready, n.one())
        vec.wait_ge(self.ready, n.now())

        def node_hot(c):
            return vec.tensor_scalar(self.onehot, m["one_up"][0:P, 0:P], self.local[:, bass.ds(c, 1)], None,
                                     ALU.is_equal)

        vec.tensor_scalar(self.local, self.local, 1.0 + P, None, ALU.add).then_inc(self.ready, n.one())
        vec.wait_ge(self.ready, n.now())
        if kind == 1:
            a, b = self.ends
            with vec.Fori(0, GEN) as c:
                s = Count(2 * c)
                z = self.coef[:, bass.ds(c, 1), :].rearrange("p o h -> p (o h)")
                vec.wait_ge(self.edge_in, 32 * c + 32)
                vec.tensor_tensor(z, a, b, ALU.add).then_inc(step, s.one())
                vec.wait_ge(step, s.now())
                vec.scalar_tensor_tensor(z, z, 0.2, z, ALU.mult, ALU.max).then_inc(step, s.one())
                vec.wait_ge(step, s.now())
                vec.sem_inc(self.edge_read, 1)
            with vec.Fori(0, TILES) as t:
                vec.tensor_scalar(self.local, self.local, -float(P), None, ALU.add)
                vec.drain()
                with vec.Fori(0, GEN) as c:
                    k = GEN * t + c
                    s = Count(2 * GEN + 8 * k)
                    best = self.best[:, at(t), :].rearrange("p o h -> p (o h)")
                    node_hot(c).then_inc(step, s.one())
                    vec.wait_ge(step, s.now())
                    vec.tensor_scalar(self.low, self.onehot, -1.0, 3e38, ALU.add, ALU.mult).then_inc(step, s.one())
                    vec.wait_ge(step, s.now())
                    for h in range(HEADS):
                        vec.tensor_scalar(self.logits[:, h, :], self.low, self.coef[:, bass.ds(c, 1), h], None,
                                          ALU.add).then_inc(step, s.one())
                    vec.wait_ge(step, s.now())
                    vec.sem_inc(self.apart, 1)
                    vec.wait_ge(self.turned, CREDIT + k + 1)
                    vec.tensor_reduce(self.found, self.bank[0:P, 0:HEADS * P].rearrange("p (h n) -> p h n", n=P), AX.X,
                                      ALU.max).then_inc(step, s.one())
                    vec.wait_ge(step, s.now())
                    vec.tensor_tensor(best, best, self.found, ALU.max).then_inc(step, s.one())
                    vec.wait_ge(step, s.now())
            vec.sem_inc(self.best_in, 1)
            with vec.Fori(0, GEN) as c:
                z = self.coef[:, bass.ds(c, 1), :].rearrange("p o h -> p (o h)")
                vec.wait_ge(self.top_in, 16 * c + 16)
                vec.tensor_tensor(z, z, a, ALU.subtract).then_inc(self.above, 1)
                vec.wait_ge(self.weights, CREDIT + c + 1)
            vec.tensor_scalar(self.local, self.local, float(P * TILES), None, ALU.add)
            vec.drain()
        chunks_before = (2 + 8 * TILES) * GEN if kind == 1 else 0
        for third, (first, count) in enumerate(THIRDS):
            with vec.Fori(0, count) as t:
                vec.tensor_scalar(self.local, self.local, -float(P), None, ALU.add)
                vec.drain()
                with vec.Fori(0, GEN) as c:
                    k = GEN * (t + first) + c
                    s = Count(chunks_before + 2 * k)
                    vec.wait_ge(self.row_in[third], 16 * (GEN * t + c) + 16)
                    vec.wait_ge(self.added, CREDIT + k)
                    node_hot(c).then_inc(step, s.one())
                    vec.tensor_tensor(
                        self.scaled.rearrange("p (h e) -> p h e", e=HX), self.row.rearrange("p (h e) -> p h e", e=HX),
                        self.coef[:, bass.ds(c, 1), :].rearrange("p o (h e) -> p (o h) e", e=1).to_broadcast(
                            [P, HEADS, HX]), ALU.mult).then_inc(step, s.one())
                    vec.wait_ge(step, s.now())
                    vec.sem_inc(self.message, 1)
                vec.wait_ge(self.added, CREDIT + GEN * (t + first) + GEN)
                self.fin.tile(vec, t + first, 0)

    def scalar(self, act):
        if self.kind == 1:
            with act.Fori(0, GEN) as c:
                z = self.coef[:, bass.ds(c, 1), :].rearrange("p o h -> p (o h)")
                act.wait_ge(self.above, c + 1)
                act.activation(z, z, ACT.Exp).then_inc(self.weights, 1)

    def tensor(self, pe):
        if self.kind == 1:
            with pe.Fori(0, TILES * GEN) as k:
                pe.wait_ge(self.apart, k + 1)
                for h in range(HEADS):
                    last = pe.transpose(self.bank[0:P, h * P:(h + 1) * P], self.logits[:, h, :],
                                        self.m["ident"][0:P, 0:P])
                last.then_inc(self.turned, 1)
        pe.wait_ge(self.ready, 4)
        with pe.Fori(0, TILES) as t:
            pe.wait_ge(self.fin.sums_used, CREDIT + t)
            pe.matmul(self.sums[:, 0:FX], self.zero[:, 0:P], self.zero[:, 0:FX], start=True, stop=False,
                      skip_group_check=True)
            with pe.Fori(0, GEN) as c:
                pe.wait_ge(self.message, CREDIT + GEN * t + c + 1)
                pe.matmul(self.sums[:, 0:FX], self.onehot, self.scaled, start=False, stop=True,
                          skip_group_check=True).then_inc(self.added, 1)

    def sync(self, sync):
        sync.nop()


def sum_layer(nc, m, d, kind):
    with ExitStack() as ctx:
        def sem(name):
            return ctx.enter_context(nc.semaphore(f"{name}_{kind}"))

        hot = sem("hot")
        hot_pool = sem("hot_pool")
        block_done = sem("block_done")
        block_kept = sem("block_kept")
        summed = sem("summed")
        words = TILES * P // 2 + 1

        def area(n):
            part = m["arena"][:, n * words:(n + 1) * words].bitcast(BF16)
            return part[:, 0:TILES * P].rearrange("p (i n) -> p i n", n=P)

        by_source, by_target = area(0), area(1)
        by_pool = (2, 5, 7)
        ids = [ctx.enter_context(nc.sbuf_tensor(f"ids_{kind}_{i}", [128, 4], F32)) for i in range(3)]
        kept = [ctx.enter_context(nc.sbuf_tensor(f"kept_{kind}_{i}", [P, 4, P], F32R)) for i in range(2)]
        dense = [ctx.enter_context(nc.psum_tensor(f"dense_{kind}_{i}", [P, 512], F32)) for i in range(2)]
        sums = [ctx.enter_context(nc.psum_tensor(f"sums_{kind}_{i}", [P, 512], F32)) for i in range(2)]
        fin = Finish(nc, ctx, m, kind, sums)
        slow = General(nc, ctx, m, d, kind, sums, fin)
        rows, columns = (by_source, by_target) if kind == 2 else (by_target, by_source)
        block = ctx.enter_context(nc.Block())

        @block.vector
        def _(vec):
            def onehots(t, g):
                i, n = GROUPS[g]

                def of_bucket(k):
                    if kind == 2:
                        one = m["table"][:, k, i:i + n, at(t)]
                    else:
                        one = m["table"][:, k, at(t), i:i + n].rearrange("p o (n b) -> p (o n) b", b=1)
                    return one.to_broadcast([128, n, P])

                nodes = m["one_up"][:, 0:P].rearrange("p (o n) -> p o n", o=1).to_broadcast([128, n, P])
                vec.wait_ge(block_done, 8 * t + (CREDIT - 7 + g))
                if g not in by_pool:
                    vec.tensor_tensor(by_target[:, i:i + n, :], of_bucket(1), nodes, ALU.is_equal)
                vec.tensor_tensor(by_source[:, i:i + n, :], of_bucket(0), nodes, ALU.is_equal).then_inc(hot, 1)

            def finish(last, slot, k):
                if last is not None and k < fin.parts:
                    if k == 0:
                        vec.wait_ge(summed, 8 * last + (CREDIT + 8))
                    fin.part(vec, k, last, slot)

            def tile(t, slot, last, more):
                for g in range(8):
                    if more:
                        onehots(t + 1, g)
                    if g < 7:
                        finish(last, 1 - slot, g)
                    if g == 6:
                        finish(last, 1 - slot, 7)
                finish(last, 1 - slot, 8)

            vec.sem_inc(block_done, CREDIT)
            fin.start(vec)
            with fast(vec, m, 0):
                for g in range(8):
                    onehots(0, g)
                with_last(vec, tile)
                for k in range(fin.parts):
                    finish(TILES - 1, 0, k)
            with vec.Else():
                slow.vector(vec)
            vec.nop()

        @block.tensor
        def _(pe):
            def blocks(t, g):
                q, (i, n) = 8 * t + g, GROUPS[g]
                pe.wait_ge(hot, 8 * t + (g + 1))
                if g in by_pool:
                    pe.wait_ge(hot_pool, len(by_pool) * t + (by_pool.index(g) + 1))
                pe.wait_ge(block_kept, CREDIT + q - 1)
                for b in range(n):
                    last = pe.matmul(dense[g % 2][:, b * P:(b + 1) * P], rows[:, i + b, :], columns[:, i + b, :],
                                     start=True, stop=True)
                last.then_inc(block_done, 1)

            def products(t, slot, g):
                q, (i, n) = 8 * t + g, GROUPS[g]
                pe.wait_ge(block_kept, CREDIT + q + 1)
                if g == 0:
                    pe.wait_ge(fin.sums_used, CREDIT + t - 1)
                for b in range(n):
                    for part in range(2):
                        last = pe.matmul(sums[slot][:, 0:FX], kept[g % 2][:, b, :], m["hs"][:, part, i + b, :],
                                         start=i + b == 0 and part == 0, stop=i + b == TILES - 1 and part == 1)
                last.then_inc(summed, 1)

            def tile(t, slot, more):
                for g in range(8):
                    if g < 7:
                        blocks(t, g + 1)
                    elif more:
                        blocks(t + 1, 0)
                    products(t, slot, g)

            pe.sem_inc(summed, CREDIT)
            with fast(pe, m, 0):
                blocks(0, 0)
                in_pairs(pe, tile)
            with pe.Else():
                slow.tensor(pe)
            pe.nop()

        @block.scalar
        def _(act):
            def keep(t, g):
                q, n = 8 * t + g, GROUPS[g][1]
                act.wait_ge(block_done, CREDIT + q + 1)
                act.wait_ge(summed, CREDIT + q - 1)
                act.copy(kept[g % 2][:, 0:n, :], dense[g % 2][:, 0:n * P].rearrange("p (b n) -> p b n", n=P)
                         ).then_inc(block_kept, 1)

            def tile(t, slot, more):
                for g in range(8):
                    keep(t, g)

            act.sem_inc(block_kept, CREDIT)
            with fast(act, m, 0):
                in_pairs(act, tile)
            with act.Else():
                slow.scalar(act)
            act.nop()

        @block.gpsimd
        def _(pool):
            if kind == 2:
                pool.tensor_tensor(m["x"][:, :, :], m["x"][:, :, :],
                                   m["bias2"][:, :].rearrange("p (o f) -> p o f", o=1).to_broadcast([P, TILES, F]),
                                   ALU.add)
            def onehots(t, n_th, g):
                i, n = GROUPS[g]
                pool.wait_ge(block_done, 8 * t + (CREDIT - 7 + g))
                if kind == 2:
                    targets = m["table"][:, 1, i:i + n, at(t)].rearrange("p n o -> p (n o)")
                else:
                    targets = m["table"][:, 1, at(t), i:i + n].rearrange("p o n -> p (o n)")
                pool.tensor_copy(ids[n_th][:, 0:n], targets)
                pool.drain()
                for b in range(n):
                    last = pool.tensor_scalar(by_target[:, i + b, :], m["one_up"][:, 0:P], ids[n_th][:, b:b + 1], None,
                                              ALU.is_equal)
                last.then_inc(hot_pool, 1)

            def tile(t, slot, last, more):
                for n_th, g in enumerate(by_pool):
                    if kind == 3 and last is not None and g == 7:
                        fin.root(pool, last)
                    if more:
                        onehots(t + 1, n_th, g)

            with fast(pool, m, 0):
                for n_th, g in enumerate(by_pool):
                    onehots(0, n_th, g)
                with_last(pool, tile)
                if kind == 3:
                    fin.root(pool, TILES - 1)
            with pool.Else():
                slow.gpsimd(pool)
            pool.nop()


def edge_layer(nc, m, d, kind):
    with ExitStack() as ctx:
        def sem(name):
            return ctx.enter_context(nc.semaphore(f"{name}_{kind}"))

        def sb(name, shape, dt=F32):
            return ctx.enter_context(nc.sbuf_tensor(f"{name}_{kind}", shape, dt))

        rows_in = [sem(f"rows_in{h}") for h in range(2)]
        edges_hot = sem("edges_hot")
        turned = sem("turned")
        nodes_hot = sem("nodes_hot")
        weights = sem("weights")
        gathered = sem("gathered")
        scaled = sem("scaled")
        firsts = sem("firsts")
        seconds = sem("seconds")
        summed = sem("summed")
        if kind == 1:
            seconds_pool = sem("seconds_pool")
            logits_done = sem("logits_done")
            logits_read = sem("logits_read")
            step = sem("step")
            exponent = sem("exponent")
        room = 13 * 128 // 2
        arena = m["arena"]

        def part(n, count, dt):
            return arena[0:P, n * room:(n + count) * room].bitcast(dt)

        rows = {(k, h): part(2 * k + h, 1, BF16) for k in range(2) for h in range(2)}
        from_source = [part(4 + h, 1, BF16) for h in range(2)]
        from_target = [sb(f"from_target{h}", [P, 13 * RANKS], F32R) for h in range(2)]
        to_nodes = sb("to_nodes", [128, TILES, P], F32R)
        columns = HEADS if kind == 1 else 1
        SLOTS = 4 if kind == 1 else 5
        scale = [sb(f"scale{h}", [128, 13, columns]) for h in range(2)]
        message = [sb(f"message{i}", [128, FX]) for i in range(10)] if kind == 1 else None
        first = [sb(f"first{i}", [128, FX], F32R) for i in range(10)]
        second = [sb(f"second{i}", [128, FX], F32R) for i in range(10)]
        sums = [ctx.enter_context(nc.psum_tensor(f"sums_{kind}_{i}", [P, 512], F32)) for i in range(2)]
        edge_rows = [ctx.enter_context(nc.psum_tensor(f"edge_rows_{kind}_{i}", [128, 512], F32)) for i in range(SLOTS)]
        turn = ctx.enter_context(nc.psum_tensor(f"turn_{kind}", [128, 8, 128], BF16))
        edge_logits = None
        if kind == 1:
            edge_logits = ctx.enter_context(nc.psum_tensor("edge_logits", [128, 512], F32))
            logits = [sb(f"logits{h}", [128, 13, 12]) for h in range(2)]
            expo = [sb(f"expo{h}", [128, 13, HEADS]) for h in range(2)]
            parts = edge_logits[:, 0:13 * 36].rearrange("p (i s c) -> p i s c", s=3, c=12)
        fin = Finish(nc, ctx, m, kind, sums)
        slow = General(nc, ctx, m, d, kind, sums, fin, edge_logits)
        block = ctx.enter_context(nc.Block())
        turns = [[(0, 6), (6, 6)], [(0, 7), (7, 6)]]
        own = (3, 11, 15, 22) if kind == 1 else tuple(range(TILES))
        fin_at = dict(zip([6, 7, 8, 9, 11, 12, 14] if kind == 1 else [6, 8, 9, 11, 14], range(fin.parts - 1)))
        fin_at |= {18: fin.parts - 1}
        root_at = 15

        def half_of(i):
            return (0, i) if i < HALF[0] else (1, i - HALF[0])

        def following(t, half):
            return (t, 1) if half == 0 else (t + 1, 0)

        def number(t, i):
            return TILES * t + (33 + i)

        def wait_second(eng, t, i):
            i, t_base = (i, 0) if i >= 0 else (i + TILES, -1)
            mine = sum(1 for k in own if k <= i)
            if i in own:
                eng.wait_ge(seconds, len(own) * t + (32 + mine + t_base * len(own)))
            else:
                others = TILES - len(own)
                eng.wait_ge(seconds_pool, others * t + (32 + i + 1 - mine + t_base * others))

        def spot(slot, i):
            return (5 * slot + i) % 10

        @block.sync
        def _(sync):
            def load(t, half):
                i, n = START[half], HALF[half]
                sync.wait_ge(edges_hot, CREDIT + 6 * t + 3 * half - 3)
                for k in range(2):
                    sync.dma_start(rows[k, half][:, 0:n * RANKS],
                                   d["rows"][k, bass.ds(TILES * t + i, n), :].rearrange("i r -> (i r)")
                                   .partition_broadcast(P)).then_inc(rows_in[half], 16)

            def tile(t, slot, more):
                load(t, 0)
                load(t, 1)

            with fast(sync, m, kind):
                in_pairs(sync, tile)
            with sync.Else():
                slow.sync(sync)
            sync.nop()

        @block.gpsimd
        def _(pool):
            def copy_weights(t, half):
                i, n = START[half], HALF[half]
                pool.wait_ge(seconds, TILES * t + (32 + i + n - TILES))
                pool.tensor_copy(scale[half][:, 0:n, 0], m["table"][:, 2, at(t), i:i + n].rearrange("p o n -> p (o n)")
                                 ).then_inc(weights, 1)

            def tile(t, slot, last, more):
                if kind == 0:
                    copy_weights(t, 0)
                    copy_weights(t, 1)
                    if last is not None:
                        fin.root(pool, last)
                else:
                    for i in range(TILES):
                        if last is not None and i == root_at:
                            fin.root(pool, last)
                        if i not in own:
                            pool.wait_ge(firsts, number(t, i))
                            pool.tensor_tensor(second[spot(slot, i)][:, :], message[spot(slot, i)][:, :],
                                               first[spot(slot, i)][:, :].bitcast(F32), ALU.subtract
                                               ).then_inc(seconds_pool, 1)

            with fast(pool, m, kind):
                if kind == 1:
                    pool.sem_inc(seconds_pool, 32)
                with_last(pool, tile)
                fin.root(pool, TILES - 1)
            with pool.Else():
                slow.gpsimd(pool)
            pool.nop()

        @block.vector
        def _(vec):
            def edges_onehot(t, half, piece):
                k, start, stop = [(0, 0, HALF[half]), (1, 0, 7), (1, 7, HALF[half])][piece]
                n = HALF[half]
                vec.wait_ge(rows_in[half], 32 * t + 32)
                if k == 0:
                    vec.wait_ge(turned, 4 * t + (CREDIT - 2 + 2 * half))
                    into = from_source[half]
                else:
                    vec.wait_ge(gathered, TILES * t + (32 - TILES + START[half] + n))
                    into = from_target[half]
                edges = slice(start * RANKS, stop * RANKS)
                vec.tensor_scalar(into[:, edges], rows[k, half][:, edges], m["row"][0:P, :], None, ALU.is_equal
                                  ).then_inc(edges_hot, 1)

            def exponents(t, half, k):
                n, u = HALF[half], 2 * t + half
                all_parts, e = logits[half][:, 0:n, :], expo[half][:, 0:n, :]
                if k == 0:
                    vec.wait_ge(logits_done, u + 1)
                    vec.tensor_reduce(all_parts, parts[:, 0:n, :, :].rearrange("p i s c -> p i c s"), AX.X, ALU.add
                                      ).then_inc(logits_read, 1)
                if k == 1:
                    vec.wait_ge(logits_read, CREDIT + u + 1)
                    vec.wait_ge(weights, CREDIT + u - 1)
                    vec.tensor_tensor(e, all_parts[:, :, 0:4], all_parts[:, :, 8:12], ALU.add).then_inc(step, 1)
                if k == 2:
                    vec.wait_ge(step, 2 * u + 1)
                    vec.scalar_tensor_tensor(e, e, 0.2, e, ALU.mult, ALU.max).then_inc(step, 1)
                if k == 3:
                    vec.wait_ge(step, 2 * u + 2)
                    vec.tensor_tensor(e, e, all_parts[:, :, 4:8], ALU.subtract).then_inc(exponent, 1)

            def scale_rows(t, i, slot):
                half, b = half_of(i)
                vec.wait_ge(gathered, number(t, i))
                wait_second(vec, t, i - 10)
                vec.tensor_tensor(
                    message[spot(slot, i)][:, :].rearrange("p (h e) -> p h e", e=HX),
                    edge_rows[i % SLOTS][:, 0:FX].rearrange("p (h e) -> p h e", e=HX),
                    scale[half][:, b, :].rearrange("p (h o) -> p h o", o=1).to_broadcast([128, HEADS, HX]),
                    ALU.mult).then_inc(scaled, 1)

            def second_part(t, i, slot):
                half, b = half_of(i)
                vec.wait_ge(firsts, number(t, i))
                into, of = second[spot(slot, i)][:, :], first[spot(slot, i)][:, :].bitcast(F32)
                if kind == 1:
                    vec.tensor_tensor(into, message[spot(slot, i)][:, :], of, ALU.subtract).then_inc(seconds, 1)
                else:
                    vec.scalar_tensor_tensor(into, edge_rows[i % SLOTS][:, 0:FX], scale[half][:, b, :], of, ALU.mult,
                                             ALU.subtract).then_inc(seconds, 1)

            def tile(t, slot, last, more):
                for i in range(TILES):
                    half, b = half_of(i)
                    nxt = following(t, half) if more or half == 0 else None
                    if b == 0:
                        vec.wait_ge(weights, CREDIT + 2 * t + half + 1)
                    if kind == 1:
                        scale_rows(t, i, slot)
                        if i - 2 in own:
                            second_part(t, i - 2, slot)
                    else:
                        second_part(t, i, slot)
                    if nxt and b in (0, 1, 3):
                        edges_onehot(*nxt, {0: 0, 1: 1, 3: 2}[b])
                    if nxt and kind == 1 and 8 <= b < 11:
                        exponents(*nxt, b - 8)
                        if b == 10:
                            exponents(*nxt, 3)
                    if last is not None and i in fin_at:
                        if fin_at[i] == 0:
                            vec.wait_ge(summed, number(last, TILES - 1))
                        fin.part(vec, fin_at[i], last, 1 - slot)

            vec.sem_inc(edges_hot, CREDIT)
            fin.start(vec)
            if kind == 1:
                vec.sem_inc(logits_read, CREDIT)
            with fast(vec, m, kind):
                vec.sem_inc(seconds, 32)
                vec.sem_inc(scaled, 32)
                for piece in range(3):
                    edges_onehot(0, 0, piece)
                if kind == 1:
                    for k in range(4):
                        exponents(0, 0, k)
                with_last(vec, tile)
                vec.wait_ge(summed, number(TILES - 1, TILES - 1))
                fin.tile(vec, TILES - 1, 0)
            with vec.Else():
                slow.vector(vec)
            vec.nop()

        @block.scalar
        def _(act):
            def keep_turned(t, half, group):
                i, n = turns[half][group]
                i += START[half]
                act.wait_ge(turned, 4 * t + (CREDIT + 2 * half + group + 1))
                act.wait_ge(summed, TILES * t + (32 - TILES + i + n))
                act.copy(to_nodes[:, i:i + n, :], turn[:, 0:n, 0:P]).then_inc(nodes_hot, 1)

            def exp(t, half):
                act.wait_ge(exponent, 2 * t + half + 1)
                act.activation(scale[half][:, 0:HALF[half], :], expo[half][:, 0:HALF[half], :], ACT.Exp
                               ).then_inc(weights, 1)

            def first_part(t, i, slot):
                half, b = half_of(i)
                act.wait_ge(summed, TILES * t + (33 + i - 10))
                if kind == 1:
                    act.wait_ge(scaled, number(t, i))
                    act.copy(first[spot(slot, i)][:, :], message[spot(slot, i)][:, :]).then_inc(firsts, 1)
                else:
                    if b == 0:
                        act.wait_ge(weights, CREDIT + 2 * t + half + 1)
                    act.wait_ge(gathered, number(t, i))
                    act.activation(first[spot(slot, i)][:, :], edge_rows[i % SLOTS][:, 0:FX], ACT.Copy,
                                   scale=scale[half][:, b, :]).then_inc(firsts, 1)

            def tile(t, slot, last, more):
                for i in range(TILES):
                    half, b = half_of(i)
                    nxt = following(t, half) if more or half == 0 else None
                    first_part(t, i, slot)
                    if nxt and b in (4, 8):
                        keep_turned(*nxt, 0 if b == 4 else 1)
                    if nxt and kind == 1 and b == 10:
                        exp(*nxt)

            act.sem_inc(weights, CREDIT)
            act.sem_inc(nodes_hot, CREDIT)
            with fast(act, m, kind):
                act.sem_inc(firsts, 32)
                for group in range(2):
                    keep_turned(0, 0, group)
                if kind == 1:
                    exp(0, 0)
                with_last(act, tile)
            with act.Else():
                slow.scalar(act)
            act.nop()

        @block.tensor
        def _(pe):
            def turn_sources(t, half, group):
                i, n = turns[half][group]
                pe.wait_ge(edges_hot, CREDIT + 6 * t + 3 * half + 1)
                pe.wait_ge(nodes_hot, 4 * t + (CREDIT + 2 * half + group))
                for b in range(n):
                    last = pe.transpose(turn[:, b, 0:P], from_source[half][:, (i + b) * RANKS:(i + b + 1) * RANKS],
                                        m["identb"][0:P, 0:P])
                last.then_inc(turned, 1)

            def gather_logits(t, half):
                i, n = START[half], HALF[half]
                pe.wait_ge(edges_hot, CREDIT + 6 * t + 3 * half + 3)
                pe.wait_ge(logits_read, CREDIT + 2 * t + half)
                for b in range(n):
                    edges = slice(b * RANKS, (b + 1) * RANKS)
                    pe.matmul(parts[:, b, :, 0:8], from_source[half][:, edges],
                              m["logit"][:, at(t), :, 0:8].rearrange("p o s c -> p (o s) c"), start=True, stop=True)
                    last = pe.matmul(parts[:, b, :, 8:12], from_target[half][:, edges],
                                     m["logit_r"][:, i + b, :, :], start=True, stop=True)
                last.then_inc(logits_done, 1)

            def gather(t, i):
                half, b = half_of(i)
                if b in (0, 7):
                    pe.wait_ge(edges_hot, CREDIT + 6 * t + 3 * half + (2 if b == 0 else 3))
                back = SLOTS if kind == 0 or i >= SLOTS else (1 if i == 0 else 5)
                pe.wait_ge(scaled if kind == 1 else seconds, TILES * t + (33 + i - back))
                for part in range(2):
                    last = pe.matmul(edge_rows[i % SLOTS][:, 0:FX], from_target[half][:, b * RANKS:(b + 1) * RANKS],
                                     m["hs"][:, part, i, :], start=part == 0, stop=part == 1)
                last.then_inc(gathered, 1)

            def add(t, i, slot):
                half, b = half_of(i)
                pe.wait_ge(nodes_hot, 4 * t + (CREDIT + 2 * half + (b >= turns[half][1][0]) + 1))
                if i == 0:
                    pe.wait_ge(fin.sums_used, CREDIT + t - 1)
                pe.wait_ge(firsts, number(t, i))
                wait_second(pe, t, i)
                for n, message_part in enumerate((first, second)):
                    last = pe.matmul(sums[slot][:, 0:FX], to_nodes[:, i, :], message_part[spot(slot, i)][:, :],
                                     start=i == 0 and n == 0, stop=i == TILES - 1 and n == 1)
                last.then_inc(summed, 1)

            def tile(t, slot, last, more):
                for i in range(TILES):
                    half, b = half_of(i)
                    nxt = following(t, half) if more or half == 0 else None
                    gather(t, i)
                    if i >= LAG:
                        add(t, i - LAG, slot)
                    elif last is not None:
                        add(last, TILES + i - LAG, 1 - slot)
                    if nxt and b in (4, 8):
                        turn_sources(*nxt, 0 if b == 4 else 1)
                    if nxt and kind == 1 and b == 6:
                        gather_logits(*nxt)

            pe.sem_inc(turned, CREDIT)
            with fast(pe, m, kind):
                pe.sem_inc(summed, 32)
                pe.sem_inc(gathered, 32)
                for group in range(2):
                    turn_sources(0, 0, group)
                if kind == 1:
                    gather_logits(0, 0)
                with_last(pe, tile)
                for i in range(TILES - LAG, TILES):
                    add(TILES - 1, i, 0)
            with pe.Else():
                slow.tensor(pe)
            pe.nop()


def last_layer(nc, m, d):
    with ExitStack() as ctx:
        def sem(name):
            return ctx.enter_context(nc.semaphore(f"{name}_l"))

        def sb(name, shape, n=2):
            return [ctx.enter_context(nc.sbuf_tensor(f"{name}_l{i}", shape, F32)) for i in range(n)]

        ends_in = sem("ends_in")
        rows_in = [sem(f"rows_in{g}") for g in range(5)]
        step = sem("step")
        top = sem("top")
        raised = sem("raised")
        variance = sem("variance")
        rooted = sem("rooted")
        ready = sem("ready")
        written = sem("written")
        ends = [ctx.enter_context(nc.sbuf_tensor(f"ends_l{i}", [P, TILES], I32)) for i in range(2)]
        source = ctx.enter_context(nc.sbuf_tensor("source_l", [P, TILES, HEADS], F32))
        target = m["hx"][:, :, :]
        logit, power = sb("logit", [P, 5, HEADS]), sb("power", [P, 5, HEADS])
        top_of, total, inverse = sb("top_of", [P, 5]), sb("total", [P, 5]), sb("inverse", [P, 5])
        mean, stats = sb("mean", [P, 5, 2]), sb("stats", [P, 5, 6])
        deviation = sb("deviation", [P, 5])
        scaled, = sb("scaled", [P, 5, F], 1)
        one_head, = sb("one_head", [P, 5, HD], 1)
        new = sb("new", [P, 5, F])
        block = ctx.enter_context(nc.Block())

        def by_group(t, g):
            return t[:, 5 * g:5 * g + 5, :]

        @block.sync
        def _(sync):
            with nc.allow_non_contiguous_dma(reason="12.5 KB each, once"):
                sync.dma_start(ends[0][:, :], d["src"][0:N].rearrange("(t p) -> p t", p=P)).then_inc(ends_in, 16)
                sync.dma_start(ends[1][:, :], d["dst"][0:N].rearrange("(t p) -> p t", p=P)).then_inc(ends_in, 16)
            for g in range(5):
                sync.wait_ge(ready, g + 1)
                sync.dma_start(d["out"][5 * P * g:5 * P * (g + 1), :].rearrange("(t p) f -> p t f", p=P),
                               by_group(m["x"], g)).then_inc(written, 16)
            sync.wait_ge(written, 16 * 5)

        @block.gpsimd
        def _(pool):
            def gather(g):
                for t in range(5 * g, 5 * g + 5):
                    pool.indirect_dma_start(source[:, t, :], None, d["sources"],
                                            bass.IndirectOffsetOnAxis(ends[0][:, t:t + 1], 0)).then_inc(rows_in[g], 16)
                    pool.indirect_dma_start(target[:, t, :], None, d["targets"],
                                            bass.IndirectOffsetOnAxis(ends[1][:, t:t + 1], 0)).then_inc(rows_in[g], 16)

            def root(g):
                pool.wait_ge(variance, g + 1)
                pool.tensor_tensor(deviation[g % 2][:, :], mean[g % 2][:, :, 1],
                                   m["minus_half"][:, :].to_broadcast([P, 5]), ALU.pow).then_inc(rooted, 1)

            pool.wait_ge(ends_in, 32)
            gather(0)
            for g in range(1, 5):
                gather(g)
                root(g - 1)
            root(4)

        @block.scalar
        def _(act):
            for g in range(5):
                act.wait_ge(top, g + 1)
                act.activation(power[g % 2][:, :, :], logit[g % 2][:, :, :], ACT.Exp).then_inc(raised, 1)

        @block.vector
        def _(vec):
            s = Count()

            def exponents(g):
                z, t = logit[g % 2][:, :, :], top_of[g % 2][:, :]
                rows = by_group(target, g).rearrange("p t (h e) -> p t h e", e=HX)
                vec.wait_ge(rows_in[g], 16 * 10)
                vec.tensor_tensor(z, by_group(source, g), rows[:, :, :, HD], ALU.add).then_inc(step, s.one())
                vec.wait_ge(step, s.now())
                vec.scalar_tensor_tensor(z, z, 0.01, z, ALU.mult, ALU.max).then_inc(step, s.one())
                vec.wait_ge(step, s.now())
                vec.tensor_reduce(t, z, AX.X, ALU.max).then_inc(step, s.one())
                vec.wait_ge(step, s.now())
                vec.tensor_tensor(z, z, t.rearrange("p (t o) -> p t o", o=1).to_broadcast([P, 5, HEADS]),
                                  ALU.subtract).then_inc(top, 1)

            def combine(g):
                w, k = power[g % 2][:, :, :], inverse[g % 2][:, :]
                rows = by_group(target, g).rearrange("p t (h e) -> p t h e", e=HX)
                split_heads = scaled[:, :, :].rearrange("p t (h d) -> p t h d", d=HD)
                vec.wait_ge(raised, g + 1)
                vec.tensor_reduce(total[g % 2][:, :], w, AX.X, ALU.add).then_inc(step, s.one())
                vec.wait_ge(step, s.now())
                vec.reciprocal(k, total[g % 2][:, :]).then_inc(step, s.one())
                vec.wait_ge(step, s.now())
                vec.tensor_tensor(w, w, k.rearrange("p (t o) -> p t o", o=1).to_broadcast([P, 5, HEADS]), ALU.mult
                                  ).then_inc(step, s.one())
                vec.wait_ge(step, s.now())
                vec.tensor_tensor(split_heads, rows[:, :, :, 0:HD],
                                  w.rearrange("p t (h o) -> p t h o", o=1).to_broadcast([P, 5, HEADS, HD]), ALU.mult
                                  ).then_inc(step, s.one())
                vec.wait_ge(step, s.now())
                vec.tensor_reduce(one_head[:, :, :], split_heads.rearrange("p t h d -> p t d h"), AX.X, ALU.add
                                  ).then_inc(step, s.one())
                vec.wait_ge(step, s.now())
                vec.tensor_tensor(new[g % 2][:, :, :].rearrange("p t (h d) -> p t h d", d=HD),
                                  by_group(m["x"], g).rearrange("p t (h d) -> p t h d", d=HD),
                                  one_head[:, :, :].rearrange("p t (o d) -> p t o d", o=1).to_broadcast(
                                      [P, 5, HEADS, HD]), ALU.add).then_inc(step, s.one())
                vec.wait_ge(step, s.now())
                for t in range(5):
                    vec.bn_stats(stats[g % 2][:, t, :], new[g % 2][:, t, :])
                vec.drain()
                for t in range(5):
                    vec.bn_aggr(mean[g % 2][:, t, :], stats[g % 2][:, t, :])
                vec.drain()
                vec.tensor_scalar(mean[g % 2][:, :, 1], mean[g % 2][:, :, 1], EPS, None, ALU.add
                                  ).then_inc(variance, 1)

            def normalize(g):
                vec.wait_ge(rooted, g + 1)
                for t in range(5):
                    last = vec.tensor_scalar(m["x"][:, 5 * g + t, :], new[g % 2][:, t, :], mean[g % 2][:, t, 0:1],
                                             deviation[g % 2][:, t:t + 1], ALU.subtract, ALU.mult)
                last.then_inc(ready, 1)

            exponents(0)
            for g in range(5):
                combine(g)
                if g < 4:
                    exponents(g + 1)
                normalize(g)


def program(nc, d):
    with ExitStack() as ctx:
        m = tensors(nc, ctx)
        load_and_starts(nc, m, d)
        build_table(nc, m, d)
        project(nc, m, 0, 0, split=True)
        edge_layer(nc, m, d, 0)
        project(nc, m, 1, 1, split=True, attn=0)
        attention_inputs(nc, m)
        edge_layer(nc, m, d, 1)
        project(nc, m, 2, 2, split=True)
        sum_layer(nc, m, d, 2)
        split_edges(nc, m)
        sum_layer(nc, m, d, 3)
        project(nc, m, 3, 3, split=False, attn=2, d=d)
        last_layer(nc, m, d)


_INS = {"x": "x", "src": "src", "dst": "dst", "ew": "edge_weight", "nv": "node_vec", "w0": "L0_gnn_kernel",
        "bias0": "L0_gnn_bias", "w1": "L1_gnn_W", "al1": "L1_gnn_a_l", "ar1": "L1_gnn_a_r", "w2": "L2_gnn_W",
        "bias2": "L2_gnn_b", "w3": "L3_gnn_weight", "al3": "L3_gnn_attn_l", "ar3": "L3_gnn_attn_r"}
_SCRATCH = {"rows": ((2, TILES * TILES, RANKS), BF16), "targets": ((N, FX), F32),
            "sources": ((N, HEADS), F32), "halves": ((N, HEADS), F32),
            "tops": ((N, HEADS), F32)}


def kernel(**inputs):
    import numpy as _np
    import concourse.bacc as _bacc
    from concourse import mybir as _mybir
    from concourse.bass_utils import run_bass_kernel_spmd as _run

    nc = _bacc.Bacc("TRN2", target_bir_lowering=False, num_devices=1)
    arrays, d = {}, {}
    for short, name in _INS.items():
        a = _np.ascontiguousarray(inputs[name])
        if short[:2] in ("al", "ar"):
            a = a.reshape(-1)
        arrays[f"in_{short}"] = a
        d[short] = nc.dram_tensor(f"in_{short}", a.shape, _mybir.dt.from_np(a.dtype), kind="ExternalInput").ap()
    for name, (shape, dtype) in _SCRATCH.items():
        d[name] = nc.dram_tensor(f"{name}_dram", shape, dtype).ap()
    d["out"] = nc.dram_tensor("out_dram", (N, F), F32, kind="ExternalOutput").ap()
    program(nc, d)
    r = _run(nc, [arrays], core_ids=[0])
    return r.results[0]["out_dram"]
```
